# Optimizing a Trainium2 kernel written in Bass

```python
import numpy as np
import jax
import jax.numpy as jnp

def _softmax(x, axis=-1):
    return jax.nn.softmax(x, axis=axis)

def _gelu(x):
    return jax.nn.gelu(x, approximate=True)

def _silu(x):
    return jax.nn.silu(x)

def _sigmoid(x):
    return jax.nn.sigmoid(x)

def _layernorm(x, axis=-1, eps=1e-05):
    m = jnp.mean(x, axis=axis, keepdims=True)
    v = jnp.var(x, axis=axis, keepdims=True)
    return (x - m) / jnp.sqrt(v + eps)

def _scatter_add(tgt, idx, src, axis=0):
    return tgt.at[idx].add(src)

def _segment_sum(src, seg, n):
    return jax.ops.segment_sum(src, seg, n)
kernel_name = 'mk_adj_resnorm_d4_adj_r2_049c78'

def setup_inputs(seed: int=0):
    np.random.seed(seed)
    _w = jnp.asarray

    def _rec_inputs():
        import jax
        import jax.numpy as jnp
        _gk = jax.random.key(seed)
        x = -0.0001538 + 1 * jax.random.normal(jax.random.fold_in(_gk, 1), (64, 128, 384), jnp.float32)
        _a = jax.random.bernoulli(jax.random.fold_in(_gk, 2), 0.125, (64, 128, 128))
        _af = _a.astype(jnp.float32)
        _af = _af * jax.random.uniform(jax.random.fold_in(_gk, 3), (64, 128, 128), jnp.float32, 0.05, 0.999992)
        adj = _af
        return (x, adj)
    x, adj = _rec_inputs()

    def _L0_gnn_setup():
        import jax, jax.numpy as jnp
        import numpy as np
        B, N, D, H = (8, 512, 384, 12)
        HD = D // H

        def _split_heads(x):
            b, n, _ = x.shape
            return x.reshape(b, n, H, HD).transpose(0, 2, 1, 3)
        key = jax.random.key(seed)
        ks = jax.random.split(key, 10)
        input_graph = jax.random.normal(ks[0], (B, N, D), dtype=jnp.float32)
        u = jax.random.uniform(ks[1], (B, N, N), dtype=jnp.float32)
        keep = jax.random.uniform(ks[2], (B, N, N)) < 0.15
        adj = jnp.where(keep, u, 0.0)
        s = 1.0 / np.sqrt(D)
        Wq = jax.random.normal(ks[3], (D, D), dtype=jnp.float32) * s
        bq = jnp.zeros((D,), dtype=jnp.float32)
        Wk = jax.random.normal(ks[4], (D, D), dtype=jnp.float32) * s
        bk = jnp.zeros((D,), dtype=jnp.float32)
        Wv = jax.random.normal(ks[5], (D, D), dtype=jnp.float32) * s
        bv = jnp.zeros((D,), dtype=jnp.float32)
        beta = jnp.asarray(0.1, dtype=jnp.float32)
        return {'input_graph': input_graph, 'adj': adj, 'Wq': Wq, 'bq': bq, 'Wk': Wk, 'bk': bk, 'Wv': Wv, 'bv': bv, 'beta': beta}
    _L0_gnn_all = _L0_gnn_setup()
    _L0_gnn_in = {k: v for k, v in _L0_gnn_all.items() if k in ('Wq', 'bq', 'Wk', 'bk', 'Wv', 'bv', 'beta')}
    del _L0_gnn_all

    def _L1_gnn_setup():
        import jax, jax.numpy as jnp
        import numpy as np
        B, S, H, L = (32, 256, 384, 2)

        def _layer_norm(z, a, b, eps=0.001):
            mu = jnp.mean(z, axis=-1, keepdims=True)
            sigma = jnp.std(z, axis=-1, keepdims=True, ddof=1)
            return (z - mu) / (sigma + eps) * a + b
        key = jax.random.key(seed)
        ks = jax.random.split(key, 6)
        hidden_state = jax.random.normal(ks[0], (B, S, H), dtype=jnp.float32)
        adjacency_matrix = (jax.random.uniform(ks[1], (B, S, S)) < 0.2).astype(jnp.float32)
        W_left = 0.05 * jax.random.normal(ks[2], (L, H, H), dtype=jnp.float32)
        W_right = 0.05 * jax.random.normal(ks[3], (L, H, H), dtype=jnp.float32)
        W_lin = 0.05 * jax.random.normal(ks[4], (L, H, H), dtype=jnp.float32)
        b_lin = jnp.zeros((L, H), dtype=jnp.float32)
        ln_a = jnp.ones((L, H), dtype=jnp.float32)
        ln_b = jnp.zeros((L, H), dtype=jnp.float32)
        return {'hidden_state': hidden_state, 'adjacency_matrix': adjacency_matrix, 'W_left': W_left, 'W_right': W_right, 'W_lin': W_lin, 'b_lin': b_lin, 'ln_a': ln_a, 'ln_b': ln_b}
    _L1_gnn_all = _L1_gnn_setup()
    _L1_gnn_in = {k: v for k, v in _L1_gnn_all.items() if k in ('W_left', 'W_right', 'W_lin', 'b_lin', 'ln_a', 'ln_b')}
    del _L1_gnn_all

    def _L2_gnn_setup():
        import jax, jax.numpy as jnp
        import numpy as np
        LN_EPS = 1e-12

        def _digcn_forward(hidden_state, adjacency_matrix, Wl, bl, Ws, bs, Wr, br, ln_w, ln_b):
            B, S, D = hidden_state.shape
            temper = jnp.asarray(D, jnp.float32) ** 0.5
            i = jnp.arange(S)
            upper = (i[None, :] > i[:, None]).astype(hidden_state.dtype)
            lower = (i[None, :] < i[:, None]).astype(hidden_state.dtype)

            def layer(h, params):
                wl, b_l, ws, b_s, wr, b_r, g, beta = params
                u = jnp.einsum('bid,bjd->bij', h, h) / temper
                a = jax.nn.softmax(u, axis=-1)
                delta = a * adjacency_matrix
                attn = delta / (jnp.sum(delta, axis=-1, keepdims=True) + 1e-10)
                hl = h @ wl.T + b_l
                hs = h @ ws.T + b_s
                hr = h @ wr.T + b_r
                diag_a = jnp.diagonal(attn, axis1=1, axis2=2)
                ctx = jnp.einsum('bij,bjd->bid', attn * upper, hl) + diag_a[..., None] * hs + jnp.einsum('bij,bjd->bid', attn * lower, hr)
                mean = ctx.mean(-1, keepdims=True)
                var = ctx.var(-1, keepdims=True)
                o = (ctx - mean) / jnp.sqrt(var + LN_EPS) * g + beta
                return (jax.nn.relu(o), None)
            out, _ = jax.lax.scan(layer, hidden_state, (Wl, bl, Ws, bs, Wr, br, ln_w, ln_b))
            return out
        key = jax.random.key(seed)
        ks = jax.random.split(key, 6)
        B, S, D, L = (8, 512, 384, 2)
        scale = (1.0 / D) ** 0.5
        hidden_state = jax.random.normal(ks[0], (B, S, D), jnp.float32)
        adjacency_matrix = (jax.random.uniform(ks[1], (B, S, S)) < 0.05).astype(jnp.float32)
        Wl = jax.random.normal(ks[2], (L, D, D), jnp.float32) * scale
        Ws = jax.random.normal(ks[3], (L, D, D), jnp.float32) * scale
        Wr = jax.random.normal(ks[4], (L, D, D), jnp.float32) * scale
        bl = jnp.zeros((L, D), jnp.float32)
        bs = jnp.zeros((L, D), jnp.float32)
        br = jnp.zeros((L, D), jnp.float32)
        ln_w = jnp.ones((L, D), jnp.float32)
        ln_b = jnp.zeros((L, D), jnp.float32)
        return dict(hidden_state=hidden_state, adjacency_matrix=adjacency_matrix, Wl=Wl, bl=bl, Ws=Ws, bs=bs, Wr=Wr, br=br, ln_w=ln_w, ln_b=ln_b)
    _L2_gnn_all = _L2_gnn_setup()
    _L2_gnn_in = {k: v for k, v in _L2_gnn_all.items() if k in ('Wl', 'bl', 'Ws', 'bs', 'Wr', 'br', 'ln_w', 'ln_b')}
    del _L2_gnn_all

    def _L3_gnn_setup():
        import jax, jax.numpy as jnp
        import numpy as np
        NUM_HEADS = 12
        HIDDEN = 384
        HEAD = HIDDEN // NUM_HEADS
        SCALE = HIDDEN ** (-0.5)
        key = jax.random.key(seed)
        ks = jax.random.split(key, 8)
        B, N = (16, 256)
        std = HIDDEN ** (-0.5)
        return {'x': jax.random.normal(ks[0], (B, N, HIDDEN), dtype=jnp.float32), 'encoding_bias': jax.random.normal(ks[1], (B, N, N), dtype=jnp.float32), 'Wq': jax.random.normal(ks[2], (HIDDEN, HIDDEN), dtype=jnp.float32) * std, 'Wk': jax.random.normal(ks[3], (HIDDEN, HIDDEN), dtype=jnp.float32) * std, 'Wv': jax.random.normal(ks[4], (HIDDEN, HIDDEN), dtype=jnp.float32) * std, 'bv': jax.random.normal(ks[5], (HIDDEN,), dtype=jnp.float32) * 0.01, 'Wo': jax.random.normal(ks[6], (HIDDEN, HIDDEN), dtype=jnp.float32) * std, 'bo': jax.random.normal(ks[7], (HIDDEN,), dtype=jnp.float32) * 0.01}
    _L3_gnn_all = _L3_gnn_setup()
    _L3_gnn_in = {k: v for k, v in _L3_gnn_all.items() if k in ('Wq', 'Wk', 'Wv', 'bv', 'Wo', 'bo')}
    del _L3_gnn_all
    return {'x': x, 'adj': adj, 'L0_gnn_Wq': _L0_gnn_in['Wq'], 'L0_gnn_bq': _L0_gnn_in['bq'], 'L0_gnn_Wk': _L0_gnn_in['Wk'], 'L0_gnn_bk': _L0_gnn_in['bk'], 'L0_gnn_Wv': _L0_gnn_in['Wv'], 'L0_gnn_bv': _L0_gnn_in['bv'], 'L0_gnn_beta': _L0_gnn_in['beta'], 'L1_gnn_W_left': _L1_gnn_in['W_left'], 'L1_gnn_W_right': _L1_gnn_in['W_right'], 'L1_gnn_W_lin': _L1_gnn_in['W_lin'], 'L1_gnn_b_lin': _L1_gnn_in['b_lin'], 'L1_gnn_ln_a': _L1_gnn_in['ln_a'], 'L1_gnn_ln_b': _L1_gnn_in['ln_b'], 'L2_gnn_Wl': _L2_gnn_in['Wl'], 'L2_gnn_bl': _L2_gnn_in['bl'], 'L2_gnn_Ws': _L2_gnn_in['Ws'], 'L2_gnn_bs': _L2_gnn_in['bs'], 'L2_gnn_Wr': _L2_gnn_in['Wr'], 'L2_gnn_br': _L2_gnn_in['br'], 'L2_gnn_ln_w': _L2_gnn_in['ln_w'], 'L2_gnn_ln_b': _L2_gnn_in['ln_b'], 'L3_gnn_Wq': _L3_gnn_in['Wq'], 'L3_gnn_Wk': _L3_gnn_in['Wk'], 'L3_gnn_Wv': _L3_gnn_in['Wv'], 'L3_gnn_bv': _L3_gnn_in['bv'], 'L3_gnn_Wo': _L3_gnn_in['Wo'], 'L3_gnn_bo': _L3_gnn_in['bo']}

def reference(x, adj, L0_gnn_Wq, L0_gnn_bq, L0_gnn_Wk, L0_gnn_bk, L0_gnn_Wv, L0_gnn_bv, L0_gnn_beta, L1_gnn_W_left, L1_gnn_W_right, L1_gnn_W_lin, L1_gnn_b_lin, L1_gnn_ln_a, L1_gnn_ln_b, L2_gnn_Wl, L2_gnn_bl, L2_gnn_Ws, L2_gnn_bs, L2_gnn_Wr, L2_gnn_br, L2_gnn_ln_w, L2_gnn_ln_b, L3_gnn_Wq, L3_gnn_Wk, L3_gnn_Wv, L3_gnn_bv, L3_gnn_Wo, L3_gnn_bo):
    import jax
    import jax.numpy as jnp

    def _L0_gnn_ref(input_graph, adj, Wq, bq, Wk, bk, Wv, bv, beta):
        import jax, jax.numpy as jnp
        import numpy as np
        B, N, D, H = (8, 512, 384, 12)
        HD = D // H

        def _split_heads(x):
            b, n, _ = x.shape
            return x.reshape(b, n, H, HD).transpose(0, 2, 1, 3)
        q = _split_heads(input_graph @ Wq + bq)
        k = _split_heads(input_graph @ Wk + bk)
        v = _split_heads(input_graph @ Wv + bv)
        scores = jnp.einsum('bhqd,bhkd->bhqk', q, k) / jnp.sqrt(jnp.asarray(HD, input_graph.dtype))
        adj_e = adj[:, None, :, :]
        scores = scores + beta * adj_e
        scores = jnp.where(adj_e > 0, scores, jnp.asarray(-9000000000000000.0, scores.dtype))
        probs = jax.nn.softmax(scores, axis=-1)
        out = jnp.einsum('bhqk,bhkd->bhqd', probs, v)
        return out.transpose(0, 2, 1, 3).reshape(input_graph.shape[0], input_graph.shape[1], D)

    def _L1_gnn_ref(hidden_state, adjacency_matrix, W_left, W_right, W_lin, b_lin, ln_a, ln_b):
        import jax, jax.numpy as jnp
        import numpy as np
        B, S, H, L = (32, 256, 384, 2)

        def _layer_norm(z, a, b, eps=0.001):
            mu = jnp.mean(z, axis=-1, keepdims=True)
            sigma = jnp.std(z, axis=-1, keepdims=True, ddof=1)
            return (z - mu) / (sigma + eps) * a + b
        temper = float(np.sqrt(H))
        adj = adjacency_matrix
        adj_tri = jnp.triu(adj, k=1)
        diag_mask = jnp.triu(adj, k=0) - adj_tri
        h = hidden_state
        for l in range(L):
            m_left = jnp.einsum('bsh,oh->bso', h, W_left[l])
            m_right = jnp.einsum('bsh,oh->bso', h, W_right[l])
            u_left = jnp.einsum('bih,bjh->bij', h, m_left) / temper
            u_right = jnp.einsum('bih,bjh->bij', h, m_right) / temper
            u = u_left * adj_tri + u_left * diag_mask + u_right * jnp.swapaxes(adj_tri, 1, 2)
            delta_exp_u = jnp.exp(u) * adj
            attention = delta_exp_u / (jnp.sum(delta_exp_u, axis=2, keepdims=True) + 1e-10)
            h_lin = jnp.einsum('bsh,oh->bso', h, W_lin[l]) + b_lin[l]
            ctx = jnp.matmul(attention, h_lin)
            h = jax.nn.relu(_layer_norm(ctx, ln_a[l], ln_b[l]))
        return h

    def _L2_gnn_ref(hidden_state, adjacency_matrix, Wl, bl, Ws, bs, Wr, br, ln_w, ln_b):
        import jax, jax.numpy as jnp
        import numpy as np
        LN_EPS = 1e-12

        def _digcn_forward(hidden_state, adjacency_matrix, Wl, bl, Ws, bs, Wr, br, ln_w, ln_b):
            B, S, D = hidden_state.shape
            temper = jnp.asarray(D, jnp.float32) ** 0.5
            i = jnp.arange(S)
            upper = (i[None, :] > i[:, None]).astype(hidden_state.dtype)
            lower = (i[None, :] < i[:, None]).astype(hidden_state.dtype)

            def layer(h, params):
                wl, b_l, ws, b_s, wr, b_r, g, beta = params
                u = jnp.einsum('bid,bjd->bij', h, h) / temper
                a = jax.nn.softmax(u, axis=-1)
                delta = a * adjacency_matrix
                attn = delta / (jnp.sum(delta, axis=-1, keepdims=True) + 1e-10)
                hl = h @ wl.T + b_l
                hs = h @ ws.T + b_s
                hr = h @ wr.T + b_r
                diag_a = jnp.diagonal(attn, axis1=1, axis2=2)
                ctx = jnp.einsum('bij,bjd->bid', attn * upper, hl) + diag_a[..., None] * hs + jnp.einsum('bij,bjd->bid', attn * lower, hr)
                mean = ctx.mean(-1, keepdims=True)
                var = ctx.var(-1, keepdims=True)
                o = (ctx - mean) / jnp.sqrt(var + LN_EPS) * g + beta
                return (jax.nn.relu(o), None)
            out, _ = jax.lax.scan(layer, hidden_state, (Wl, bl, Ws, bs, Wr, br, ln_w, ln_b))
            return out
        return _digcn_forward(hidden_state, adjacency_matrix, Wl, bl, Ws, bs, Wr, br, ln_w, ln_b)

    def _L3_gnn_ref(x, encoding_bias, Wq, Wk, Wv, bv, Wo, bo):
        import jax, jax.numpy as jnp
        import numpy as np
        NUM_HEADS = 12
        HIDDEN = 384
        HEAD = HIDDEN // NUM_HEADS
        SCALE = HIDDEN ** (-0.5)
        B, N, _ = x.shape
        q = (x @ Wq.T).reshape(B, N, NUM_HEADS, HEAD)
        k = (x @ Wk.T).reshape(B, N, NUM_HEADS, HEAD)
        v = (x @ Wv.T + bv).reshape(B, N, NUM_HEADS, HEAD)
        a = jnp.einsum('bnhd,bmhd->bhnm', q, k) * SCALE + encoding_bias[:, None, :, :]
        pad_mask = jnp.all(a == 0, axis=-1)
        a = jnp.where(pad_mask[..., None], -jnp.inf, a)
        a = jax.nn.softmax(a, axis=-1)
        a = jnp.nan_to_num(a)
        o = jnp.einsum('bhnm,bmhd->bnhd', a, v).reshape(B, N, HIDDEN)
        return o @ Wo.T + bo
    x = _layernorm(x + _L0_gnn_ref(x, adj, L0_gnn_Wq, L0_gnn_bq, L0_gnn_Wk, L0_gnn_bk, L0_gnn_Wv, L0_gnn_bv, L0_gnn_beta), axis=-1)
    x = _layernorm(x + _L1_gnn_ref(x, adj, L1_gnn_W_left, L1_gnn_W_right, L1_gnn_W_lin, L1_gnn_b_lin, L1_gnn_ln_a, L1_gnn_ln_b), axis=-1)
    x = _layernorm(x + _L2_gnn_ref(x, adj, L2_gnn_Wl, L2_gnn_bl, L2_gnn_Ws, L2_gnn_bs, L2_gnn_Wr, L2_gnn_br, L2_gnn_ln_w, L2_gnn_ln_b), axis=-1)
    x = _layernorm(x + _L3_gnn_ref(x, adj, L3_gnn_Wq, L3_gnn_Wk, L3_gnn_Wv, L3_gnn_bv, L3_gnn_Wo, L3_gnn_bo), axis=-1)
    return x

_drawn_inputs = setup_inputs


def setup_inputs(seed=0):
    import zlib

    import numpy as np

    out = dict(_drawn_inputs(seed))
    spreads = {'L0_gnn_bq': (0.0, 0.1),
     'L0_gnn_bk': (0.0, 0.8),
     'L0_gnn_bv': (0.0, 0.1),
     'L1_gnn_b_lin': (0.0, 0.1),
     'L1_gnn_ln_a': (1.0, 0.2),
     'L1_gnn_ln_b': (0.0, 0.1),
     'L2_gnn_bl': (0.0, 0.1),
     'L2_gnn_bs': (0.0, 0.274),
     'L2_gnn_br': (0.0, 0.1),
     'L2_gnn_ln_w': (1.0, 0.2),
     'L2_gnn_ln_b': (0.0, 0.1)}
    factors = {'L3_gnn_Wq': 2.885, 'L3_gnn_Wk': 2.809, 'L3_gnn_bv': 5.945, 'L3_gnn_bo': 6.566}
    for name, (base, spread) in spreads.items():
        noise = np.random.default_rng([zlib.crc32(name.encode()), seed]).standard_normal(out[name].shape)
        drawn = base * np.exp(spread * noise) if base else spread * noise
        out[name] = jnp.asarray(drawn.astype(out[name].dtype))
    for name, factor in factors.items():
        out[name] = (out[name] * factor).astype(out[name].dtype)
    return out
```

```python
import numpy as np
import concourse.bass as bass
from concourse import mybir
from contextlib import ExitStack

F32, F16 = mybir.dt.float32, mybir.dt.float16
ACT = mybir.ActivationFunctionType
ALU = mybir.AluOpType
AX = mybir.AxisListType

B, N, D = 64, 128, 384
H, HD = 12, 32
DT = D // 128
HG = 128 // HD
HS = HD + 1
UNITS = 2
ROUNDS = B // UNITS
WSCALE = 64.0
MASKED = -9000000000000000.0
TEMPER = float(np.sqrt(D))
BANK = 512

L0_Q, L0_K, L0_V = 0, 1, 2
L1_W = ((3, 4, 5), (6, 7, 8))
L2_W = ((9, 10, 11), (12, 13, 14))
L3_Q, L3_K, L3_V, L3_O = 15, 16, 17, 18
NW = 19
BIAS_OF = {L0_Q: 0, L0_K: 1, L0_V: 2, 5: 3, 8: 4, 9: 5, 10: 6, 11: 7, 12: 8, 13: 9, 14: 10, L3_V: 11, L3_O: 12}
NB = 13
NR = 8


class Signal:

    def __init__(self, ctx, nc, name, per_round=1, step=1, primed=0):
        self.sems = [ctx.enter_context(nc.semaphore(f"{name}_{u}")) for u in range(UNITS)]
        self.per_round, self.step, self.primed = per_round, step, primed

    def prime(self, eng):
        assert self.primed == 1
        for sem in self.sems:
            eng.sem_inc(sem, 1)

    def __getitem__(self, u):
        return self.sems[u]

    def at(self, u, i, k=0):
        return self.sems[u], i * (self.per_round * self.step) + ((k + 1) * self.step + self.primed)

    def before(self, u, i):
        assert self.primed == 1
        return self.sems[u], i * (self.per_round * self.step) + 1


def graph_layers(nc, x_d, adj_d, w_d, bias_d, rows_d, beta_d, out_d):
    ctx = ExitStack()
    with ctx:
        def sb(name, shape, dt=F32):
            return ctx.enter_context(nc.sbuf_tensor(name, shape, dt))

        def per_unit(name, shape, dt=F32):
            return [sb(f"{name}_{u}", shape, dt) for u in range(UNITS)]

        def sem(name):
            return ctx.enter_context(nc.semaphore(name))

        def signal(name, per_round=1, step=1, primed=0):
            return Signal(ctx, nc, name, per_round, step, primed)

        w_hi = sb("w_hi", [128, NW, DT, D], F16)
        w_lo = sb("w_lo", [128, NW, DT, D], F16)
        w_stage = sb("w_stage", [128, 2, DT, D])
        bias_rows = sb("bias_rows", [128, NB, D], F16)
        ones = sb("ones", [128, 128], F16)
        rows = sb("rows", [128, NR, D])
        ident = sb("ident", [128, 128])
        tri = sb("tri", [128, 3, 128])
        tri_temper = sb("tri_temper", [128, 2, 128])
        beta = sb("beta", [128, 1])
        powers = sb("powers", [128, 2])

        x_in = per_unit("x_in", [128, D])
        adj_in = per_unit("adj_in", [128, N])
        adj = per_unit("adj", [128, N])
        adj_t = per_unit("adj_t", [128, N])
        mask_bias = per_unit("mask_bias", [128, N])
        mask_pair = per_unit("mask_pair", [128, 2, N])
        x = per_unit("x", [128, D])
        z = per_unit("z", [128, D])
        x_out = per_unit("x_out", [128, D])
        t_hi = per_unit("t_hi", [128, DT, N], F16)
        t_lo = per_unit("t_lo", [128, DT, N], F16)
        a_hi = per_unit("a_hi", [128, DT, N], F16)
        a_lo = per_unit("a_lo", [128, DT, N], F16)
        b_hi = per_unit("b_hi", [128, DT, N], F16)
        b_lo = per_unit("b_lo", [128, DT, N], F16)
        v_hi = per_unit("v_hi", [128, H, HS], F16)
        v_lo = per_unit("v_lo", [128, H, HS], F16)
        p_hi = per_unit("p_hi", [128, 2, DT, N], F16)
        p_lo = per_unit("p_lo", [128, 2, DT, N], F16)
        top = per_unit("top", [128, HG, DT])
        low = per_unit("low", [128, HG, DT])
        inv = per_unit("inv", [128, H])
        flag = per_unit("flag", [128, HG, DT])
        u_pair = per_unit("u_pair", [128, 2, N])
        e = per_unit("e", [128, N])
        delta = per_unit("delta", [128, N])
        small = per_unit("small", [128, 12])
        VAR, ROOT, DENOM, INV, INV2, BASE, GAIN, TOP, UBIAS, ZSUM, DSUM, TICK = range(12)

        def col(u, c):
            return small[u][:, c:c + 1]

        sizes = {"score": 2 * DT * N, "proj": 3 * (D + 1), "delta3": 3 * N, "zc": D}
        shared = sb("shared", [128, UNITS * sum(sizes.values())])

        def share(name):
            at = UNITS * sum(v for k, v in sizes.items() if list(sizes).index(k) < list(sizes).index(name))
            return [shared[:, at + u * sizes[name]:at + (u + 1) * sizes[name]] for u in range(UNITS)]

        score = [a.rearrange("p (g t n) -> p g t n", g=2, t=DT) for a in share("score")]
        proj = [a.rearrange("p (m d) -> p m d", m=3) for a in share("proj")]
        delta3 = [a.rearrange("p (m n) -> p m n", m=3) for a in share("delta3")]
        zc = share("zc")
        bias_stage = shared[:, 0:NB * D].rearrange("p (b d) -> p b d", d=D)
        st6 = per_unit("st6", [128, 6])
        mv = per_unit("mv", [128, 2])

        b0 = [ctx.enter_context(nc.psum_tensor(f"b0_{u}", [128, BANK], F32)) for u in range(UNITS)]
        b1 = [ctx.enter_context(nc.psum_tensor(f"b1_{u}", [128, BANK], F32)) for u in range(UNITS)]
        s = [ctx.enter_context(nc.psum_tensor(f"s_{u}", [128, 2, BANK], F32)) for u in range(UNITS)]

        w_loaded = [sem("w_loaded_even"), sem("w_loaded_odd")]
        w_hi_made, w_lo_made = sem("w_hi_made"), sem("w_lo_made")
        small_loaded = sem("small_loaded")
        consts_cleared, consts_made = sem("consts_cleared"), sem("consts_made")
        dve_consts = sem("dve_consts")
        bias_hi_made, bias_made = sem("bias_hi_made"), sem("bias_made")
        bias_high_row = sem("bias_high_row")
        x_loaded = signal("x_loaded", step=16)
        adj_loaded = signal("adj_loaded", step=16)
        stored = signal("stored", step=16, primed=1)
        adjt_done = signal("adjt_done")
        turned = signal("turned", 7)
        projected = signal("projected", NW)
        scored = signal("scored", 4)
        p_turned = signal("p_turned", 4)
        attended = signal("attended", 2)
        u_done = signal("u_done", 4)
        delta_turned = signal("delta_turned", 2)
        mixed = signal("mixed", 4)
        adj_copied = signal("adj_copied", primed=1)
        t_hi_done = signal("t_hi_done", 7)
        proj_hi_done = signal("proj_hi_done", 16)
        exp_done = signal("exp_done", 4)
        p_hi_done = signal("p_hi_done", 4)
        e_done = signal("e_done", 4)
        masks_done = signal("masks_done", 5)
        t_lo_done = signal("t_lo_done", 7)
        proj_lo_done = signal("proj_lo_done", 12)
        biased = signal("biased", 4, primed=1)
        topped = signal("topped", 4)
        lowed = signal("lowed", 2)
        lessened = signal("lessened", 4)
        p_lo_done = signal("p_lo_done", 4)
        inverted = signal("inverted", 2)
        pad_step = signal("pad_step", 4)
        o_ready = signal("o_ready", 2)
        x_in_used = signal("x_in_used", primed=1)
        residual_added = signal("residual_added", 3, primed=1)
        u_masked = signal("u_masked", 2)
        u_ready = signal("u_ready", 2)
        u_topped = signal("u_topped", 2)
        u_bias_ready = signal("u_bias_ready", 2)
        delta_done = signal("delta_done", 4)
        delta3_done = signal("delta3_done", 2)
        denom_done = signal("denom_done", 4)
        denom_inverted = signal("denom_inverted", 4)
        inverse_squared = signal("inverse_squared", 4)
        stats_done = signal("stats_done", 8)
        moments_done = signal("moments_done", 8)
        variance_done = signal("variance_done", 8)
        centered = signal("centered", 4)
        gain_base = signal("gain_base", 2)
        gain_done = signal("gain_done", 4)
        inner_done = signal("inner_done", 4)
        normed = signal("normed", 4)
        root_done = signal("root_done", 8)

        ORDER = [L0_Q, L0_K, L0_V, *L1_W[0], *L1_W[1], *L2_W[0], *L2_W[1], L3_Q, L3_K, L3_V, L3_O]
        HI = {w: k for k, w in enumerate([L0_Q, L0_K, L0_V, *L1_W[0], *L1_W[1], L2_W[0][0], L2_W[0][2],
                                          L2_W[1][0], L2_W[1][2], L3_Q, L3_K, L3_V])}
        LO = {w: k for k, w in enumerate([L0_Q, L0_K, L0_V, *L1_W[0][:2], *L1_W[1][:2], L2_W[0][1], L2_W[1][1],
                                          L3_Q, L3_K, L3_V])}
        ROOTS = [1, 0, 0, 1, 1, 1, 1, 1]
        INNER_NORM = {0: 1, 1: 2, 2: 4, 3: 5}
        OUTER_NORM = {0: 0, 1: 3, 2: 6, 3: 7}
        block = ctx.enter_context(nc.Block())

        @block.sync
        def _(sp):
            stored.prime(sp)

            def load_weight(w, slot):
                sp.dma_start(w_stage[:, slot, :, :], w_d[w].rearrange("(t p) o -> p t o", p=128)).then_inc(w_loaded[slot], 16)

            sp.dma_start(beta[:, :], beta_d.partition_broadcast(128)).then_inc(small_loaded, 16)
            sp.dma_start(rows[:, :, :], rows_d.rearrange("r d -> (r d)").partition_broadcast(128)
                         .rearrange("p (r d) -> p r d", d=D)).then_inc(small_loaded, 16)
            for row in (0, 32):
                sp.dma_start(bias_stage[row:row + 1, :, :], bias_d.rearrange("(a b) d -> a b d", a=1))\
                  .then_inc(small_loaded, 16)
            load_weight(0, 0)
            load_weight(1, 1)
            with sp.Fori(1, NW // 2) as g:
                for slot in range(2):
                    sp.wait_ge(w_lo_made, g * 2 + slot - 1)
                    load_weight(g * 2 + slot, slot)
            sp.wait_ge(w_lo_made, NW - 2)
            load_weight(NW - 1, 0)

            def load(i, u):
                sp.dma_start(x_in[u][:, :], x_d[i * UNITS + u]).then_inc(x_loaded[u], 16)
                sp.dma_start(adj_in[u][:, :], adj_d[i * UNITS + u]).then_inc(adj_loaded[u], 16)

            with sp.Fori(0, ROUNDS) as i:
                for u in range(UNITS):
                    sp.wait_ge(*adj_copied.before(u, i))
                    sp.wait_ge(*x_in_used.before(u, i))
                    load(i, u)
                for u in range(UNITS):
                    sp.wait_ge(*normed.at(u, i, 3))
                    sp.dma_start(out_d[i * UNITS + u], x_out[u][:, :]).then_inc(stored[u], 16)
            for u in range(UNITS):
                sp.wait_ge(*stored.before(u, ROUNDS))

        @block.gpsimd
        def _(pool):
            pool.memset(ident[:, :], 0.0).then_inc(consts_cleared, 1)
            pool.memset(tri[:, :, :], 1.0).then_inc(consts_cleared, 1)
            pool.memset(tri_temper[:, :, :], 1.0 / TEMPER).then_inc(consts_cleared, 1)
            pool.memset(bias_rows[:, :, :], 0.0).then_inc(consts_cleared, 1)
            pool.wait_ge(consts_cleared, 4)
            pool.affine_select(out=ident[:, :], in_=ident[:, :], compare_op=ALU.not_equal, fill=1.0, base=0,
                               pattern=[[-1, 128]], channel_multiplier=1).then_inc(consts_made, 1)
            for m, op, sign in ((0, ALU.is_gt, 1), (1, ALU.is_equal, 1), (2, ALU.is_gt, -1)):
                pool.affine_select(out=tri[:, m, :], in_=tri[:, m, :], compare_op=op, fill=0.0, base=0,
                                   pattern=[[-sign, 128]], channel_multiplier=sign).then_inc(consts_made, 1)
            for m, op, sign in ((0, ALU.is_ge, 1), (1, ALU.is_gt, -1)):
                pool.affine_select(out=tri_temper[:, m, :], in_=tri_temper[:, m, :], compare_op=op, fill=0.0, base=0,
                                   pattern=[[-sign, 128]], channel_multiplier=sign).then_inc(consts_made, 1)
            pool.wait_ge(dve_consts, 2)

            with pool.Fori(0, ROUNDS) as i:
                for k, power in enumerate(ROOTS):
                    for u in range(UNITS):
                        pool.wait_ge(*variance_done.at(u, i, k))
                        pool.tensor_tensor(col(u, ROOT), col(u, VAR), powers[:, power:power + 1], ALU.pow)\
                            .then_inc(root_done[u], 1)

        @block.scalar
        def _(act):
            adj_copied.prime(act)
            act.wait_ge(small_loaded, 64)
            act.wait_ge(consts_cleared, 4)
            for row in (0, 32):
                act.activation(bias_rows[row:row + 1, :, :], bias_stage[row:row + 1, :, :], ACT.Copy, scale=WSCALE)\
                   .then_inc(bias_hi_made, 1)

            def weight_high(w, slot):
                act.activation(w_hi[:, bass.ds(w, 1), :, :].rearrange("p a t o -> p (a t o)"),
                               w_stage[:, slot, :, :].rearrange("p t o -> p (t o)"), ACT.Copy, scale=WSCALE)\
                   .then_inc(w_hi_made, 1)

            with act.Fori(0, NW // 2) as g:
                for slot in range(2):
                    act.wait_ge(w_loaded[slot], g * 16 + 16)
                    weight_high(g * 2 + slot, slot)
            act.wait_ge(w_loaded[0], 16 * (NW // 2) + 16)
            weight_high(NW - 1, 0)

            def turn_high(i, u, k):
                act.wait_ge(*turned.at(u, i, k))
                act.activation(t_hi[u][:, :, :], b0[u][:, 0:D].rearrange("p (t n) -> p t n", n=N),
                               ACT.Relu if k in (2, 4) else ACT.Copy).then_inc(t_hi_done[u], 1)

            def high(i, u, w, dst, src, scale):
                act.wait_ge(*projected.at(u, i, ORDER.index(w)))
                act.activation(dst, src, ACT.Copy, scale=scale / WSCALE).then_inc(proj_hi_done[u], 1)

            def qkv(i, u, ws, scale):
                high(i, u, ws[0], a_hi[u][:, :, :], b1[u][:, 0:D].rearrange("p (t n) -> p t n", n=N), scale)
                high(i, u, ws[1], b_hi[u][:, :, :], b0[u][:, 0:D].rearrange("p (t n) -> p t n", n=N), 1.0)
                high(i, u, ws[2], v_hi[u][:, :, 0:HD], s[u][:, 0, 0:D].rearrange("p (h n) -> p h n", n=HD), 1.0)

            def exps(i, u, k):
                act.wait_ge(*lessened.at(u, i, k))
                act.activation(score[u][:, :, :, :], score[u][:, :, :, :], ACT.Exp).then_inc(exp_done[u], 1)

            def p_high(i, u, half):
                act.wait_ge(*p_turned.at(u, i, half))
                act.activation(p_hi[u][:, :, :, :], s[u][:, :, 0:D].rearrange("p g (t n) -> p g t n", n=N),
                               ACT.Copy).then_inc(p_hi_done[u], 1)

            with act.Fori(0, ROUNDS) as i:
                for u in range(UNITS):
                    act.wait_ge(*adj_loaded.at(u, i))
                    act.wait_ge(*biased.before(u, i))
                    act.activation(adj[u][:, :], adj_in[u][:, :], ACT.Copy).then_inc(adj_copied[u], 1)
                    turn_high(i, u, 0)
                for u in range(UNITS):
                    qkv(i, u, (L0_Q, L0_K, L0_V), HD ** -0.5)
                for half in range(2):
                    for u in range(UNITS):
                        exps(i, u, half)
                    for u in range(UNITS):
                        p_high(i, u, half)
                for layer in range(2):
                    left, right, lin = L1_W[layer]
                    for u in range(UNITS):
                        turn_high(i, u, 1 + layer)
                    for u in range(UNITS):
                        high(i, u, left, a_hi[u][:, :, :], b1[u][:, 0:D].rearrange("p (t n) -> p t n", n=N), 1.0)
                        high(i, u, right, b_hi[u][:, :, :], b0[u][:, 0:D].rearrange("p (t n) -> p t n", n=N), 1.0)
                        high(i, u, lin, proj[u][:, 0, 0:D], s[u][:, 0, 0:D], 1.0)
                    for u in range(UNITS):
                        act.wait_ge(*u_ready.at(u, i, layer))
                        act.activation(e[u][:, :], e[u][:, :], ACT.Exp).then_inc(e_done[u], 1)
                for layer in range(2):
                    upper, diag, lower = L2_W[layer]
                    for u in range(UNITS):
                        turn_high(i, u, 3 + layer)
                    for u in range(UNITS):
                        act.wait_ge(*u_bias_ready.at(u, i, layer))
                        act.activation(e[u][:, :], b1[u][:, 0:N], ACT.Exp, bias=col(u, UBIAS), scale=1.0 / TEMPER,
                                       accum_out=col(u, ZSUM)).then_inc(e_done[u], 1)
                    for u in range(UNITS):
                        high(i, u, upper, proj[u][:, 0, 0:D], s[u][:, 0, 0:D], 1.0)
                        high(i, u, lower, proj[u][:, 2, 0:D], b0[u][:, 0:D], 1.0)
                for u in range(UNITS):
                    turn_high(i, u, 5)
                for u in range(UNITS):
                    qkv(i, u, (L3_Q, L3_K, L3_V), D ** -0.5)
                for half in range(2):
                    for u in range(UNITS):
                        exps(i, u, 2 + half)
                    for u in range(UNITS):
                        p_high(i, u, 2 + half)
                for u in range(UNITS):
                    turn_high(i, u, 6)

        @block.tensor
        def _(pe):
            def turn(i, u, k, src):
                for t in range(DT):
                    last = pe.transpose(b0[u][:, t * N:(t + 1) * N], src[u][:, t * 128:(t + 1) * 128], ident[:, :])
                last.then_inc(turned[u], 1)

            def project_across(i, u, w, out):
                for t in range(DT):
                    o = out[:, t * N:(t + 1) * N]
                    cols = slice(t * 128, (t + 1) * 128)
                    for k in range(DT):
                        pe.matmul(o, lhsT=w_hi[:, w, k, cols], rhs=t_hi[u][:, k, :], start=(k == 0), stop=False)
                        pe.matmul(o, lhsT=w_hi[:, w, k, cols], rhs=t_lo[u][:, k, :], start=False, stop=False)
                        last = pe.matmul(o, lhsT=w_lo[:, w, k, cols], rhs=t_hi[u][:, k, :], start=False,
                                         stop=(k == DT - 1 and w not in BIAS_OF))
                    if w in BIAS_OF:
                        last = pe.matmul(o, lhsT=bias_rows[:, BIAS_OF[w], cols], rhs=ones[:, :], start=False, stop=True)
                last.then_inc(projected[u], 1)

            def project(i, u, w, out):
                for k in range(DT):
                    pe.matmul(out, lhsT=t_hi[u][:, k, :], rhs=w_hi[:, w, k, :], start=(k == 0), stop=False)
                    pe.matmul(out, lhsT=t_hi[u][:, k, :], rhs=w_lo[:, w, k, :], start=False, stop=False)
                    pe.matmul(out, lhsT=t_lo[u][:, k, :], rhs=w_hi[:, w, k, :], start=False, stop=False)
                pe.matmul(out, lhsT=ones[:, :], rhs=bias_rows[:, BIAS_OF[w], :], start=False, stop=True)\
                  .then_inc(projected[u], 1)

            def product(out, ahi, alo, bhi, blo):
                for k in range(DT):
                    pe.matmul(out, lhsT=ahi[:, k, :], rhs=bhi[:, k, :], start=(k == 0), stop=False)
                    pe.matmul(out, lhsT=ahi[:, k, :], rhs=blo[:, k, :], start=False, stop=False)
                    last = pe.matmul(out, lhsT=alo[:, k, :], rhs=bhi[:, k, :], start=False, stop=(k == DT - 1))
                return last

            def qkv(i, u, ws):
                project_across(i, u, ws[0], b1[u])
                project_across(i, u, ws[1], b0[u])
                project(i, u, ws[2], s[u][:, 0, 0:D])

            def scores(i, u, half):
                for t in range(DT):
                    for qp, kp, n in ((a_hi, b_hi, 0), (a_hi, b_lo, 1), (a_lo, b_hi, 2)):
                        for g2 in range(2):
                            r = slice(HD * (2 * half + g2), HD * (2 * half + g2) + HD)
                            last = pe.matmul(s[u][:, g2, t * N:(t + 1) * N], lhsT=qp[u][r, t, :], rhs=kp[u][r, t, :],
                                             start=(n == 0), stop=(n == 2))
                last.then_inc(scored[u], 1)

            def turn_p(i, u, k):
                pe.wait_ge(*exp_done.at(u, i, k))
                for g2 in range(2):
                    for t in range(DT):
                        last = pe.transpose(s[u][:, g2, t * N:(t + 1) * N], score[u][:, g2, t, :], ident[:, :])
                last.then_inc(p_turned[u], 1)

            def attend(i, u, k):
                pe.wait_ge(*p_lo_done.at(u, i, k))
                for g2 in range(2):
                    for t in range(DT):
                        h = HG * t + 2 * (k % 2) + g2
                        o = b1[u][:, h * HS:(h + 1) * HS]
                        pe.matmul(o, lhsT=p_hi[u][:, g2, t, :], rhs=v_hi[u][:, h, :], start=True, stop=False)
                        pe.matmul(o, lhsT=p_hi[u][:, g2, t, :], rhs=v_lo[u][:, h, :], start=False, stop=False)
                        last = pe.matmul(o, lhsT=p_lo[u][:, g2, t, :], rhs=v_hi[u][:, h, :], start=False, stop=True)
                if k % 2:
                    last.then_inc(attended[u], 1)

            def attention(i, which, ws):
                for u in range(UNITS):
                    pe.wait_ge(*t_lo_done.at(u, i, 0 if which == 0 else 5))
                    if which == 0:
                        pe.wait_ge(*residual_added.before(u, i))
                    qkv(i, u, ws)
                for half in range(2):
                    for u in range(UNITS):
                        if half == 0:
                            pe.wait_ge(*proj_lo_done.at(u, i, LO[ws[2]]))
                        scores(i, u, half)
                    for u in range(UNITS):
                        turn_p(i, u, 2 * which + half)
                    for u in range(UNITS):
                        attend(i, u, 2 * which + half)

            pe.wait_ge(w_lo_made, NW)
            pe.wait_ge(bias_made, 1)
            pe.wait_ge(consts_made, 6)
            pe.wait_ge(dve_consts, 9)
            with pe.Fori(0, ROUNDS) as i:
                for u in range(UNITS):
                    pe.wait_ge(*x_loaded.at(u, i))
                    turn(i, u, 0, x_in)
                    pe.wait_ge(*adj_copied.at(u, i))
                    pe.transpose(s[u][:, 1, 0:N], adj[u][:, :], ident[:, :]).then_inc(adjt_done[u], 1)
                attention(i, 0, (L0_Q, L0_K, L0_V))
                for layer in range(2):
                    left, right, lin = L1_W[layer]
                    for u in range(UNITS):
                        pe.wait_ge(*(normed if layer == 0 else inner_done).at(u, i, 0))
                        turn(i, u, 1 + layer, x if layer == 0 else z)
                    for u in range(UNITS):
                        pe.wait_ge(*t_lo_done.at(u, i, 1 + layer))
                        project_across(i, u, left, b1[u])
                        project_across(i, u, right, b0[u])
                        project(i, u, lin, s[u][:, 0, 0:D])
                    for u in range(UNITS):
                        pe.wait_ge(*proj_lo_done.at(u, i, LO[right]))
                        product(s[u][:, 1, 0:N], a_hi[u], a_lo[u], t_hi[u], t_lo[u])
                        product(s[u][:, 1, N:2 * N], b_hi[u], b_lo[u], t_hi[u], t_lo[u]).then_inc(u_done[u], 1)
                    for u in range(UNITS):
                        pe.wait_ge(*proj_hi_done.at(u, i, HI[lin]))
                        pe.wait_ge(*delta_done.at(u, i, layer))
                        pe.matmul(b1[u][:, 0:D + 1], lhsT=delta[u][:, :], rhs=proj[u][:, 0, :], start=True, stop=True)\
                          .then_inc(mixed[u], 1)
                for layer in range(2):
                    upper, diag, lower = L2_W[layer]
                    for u in range(UNITS):
                        pe.wait_ge(*(normed.at(u, i, 1) if layer == 0 else inner_done.at(u, i, 2)))
                        turn(i, u, 3 + layer, x if layer == 0 else z)
                    for u in range(UNITS):
                        pe.wait_ge(*t_lo_done.at(u, i, 3 + layer))
                        product(b1[u][:, 0:N], t_hi[u], t_lo[u], t_hi[u], t_lo[u]).then_inc(u_done[u], 1)
                        project(i, u, upper, s[u][:, 0, 0:D])
                        project(i, u, diag, s[u][:, 1, 0:D])
                        project(i, u, lower, b0[u][:, 0:D])
                    for u in range(UNITS):
                        pe.wait_ge(*delta_done.at(u, i, 2 + layer))
                        pe.transpose(b1[u][:, N:2 * N], delta[u][:, :], ident[:, :]).then_inc(delta_turned[u], 1)
                    for u in range(UNITS):
                        pe.wait_ge(*proj_hi_done.at(u, i, HI[lower]))
                        pe.wait_ge(*proj_lo_done.at(u, i, LO[diag]))
                        pe.wait_ge(*delta3_done.at(u, i, layer))
                        for m in range(3):
                            last = pe.matmul(s[u][:, 0, 0:D], lhsT=delta3[u][:, m, :], rhs=proj[u][:, m, 0:D],
                                             start=(m == 0), stop=(m == 2))
                        last.then_inc(mixed[u], 1)
                for u in range(UNITS):
                    pe.wait_ge(*normed.at(u, i, 2))
                    turn(i, u, 5, x)
                attention(i, 1, (L3_Q, L3_K, L3_V))
                for u in range(UNITS):
                    pe.wait_ge(*o_ready.at(u, i, 1))
                    turn(i, u, 6, z)
                for u in range(UNITS):
                    pe.wait_ge(*t_lo_done.at(u, i, 6))
                    project(i, u, L3_O, b1[u][:, 0:D])

        @block.vector
        def _(dve):
            for first_round_may_go in (biased, x_in_used, residual_added):
                first_round_may_go.prime(dve)
            dve.memset(powers[:, 0:1], 0.5).then_inc(dve_consts, 1)
            dve.memset(powers[:, 1:2], -0.5).then_inc(dve_consts, 1)
            dve.memset(ones[:, :], 1.0).then_inc(dve_consts, 1)
            for u in range(UNITS):
                dve.memset(v_hi[u][:, :, HD:HS], 1.0).then_inc(dve_consts, 1)
                dve.memset(v_lo[u][:, :, HD:HS], 0.0).then_inc(dve_consts, 1)
            dve.wait_ge(bias_hi_made, 2)
            dve.scalar_tensor_tensor(bias_rows[32:33, :, :], bias_stage[32:33, :, :], WSCALE, bias_rows[32:33, :, :],
                                     ALU.mult, ALU.subtract).then_inc(bias_made, 1)
            dve.wait_ge(bias_made, 1)
            for u in range(UNITS):
                dve.memset(proj[u][:, 0, D:D + 1], 1.0).then_inc(dve_consts, 1)

            def weight_low(w, slot):
                at = bass.ds(w, 1)
                dve.scalar_tensor_tensor(w_lo[:, at, :, :].rearrange("p a t o -> p (a t o)"),
                                         w_stage[:, slot, :, :].rearrange("p t o -> p (t o)"), WSCALE,
                                         w_hi[:, at, :, :].rearrange("p a t o -> p (a t o)"),
                                         ALU.mult, ALU.subtract).then_inc(w_lo_made, 1)

            with dve.Fori(0, NW // 2) as g:
                for slot in range(2):
                    dve.wait_ge(w_hi_made, g * 2 + slot + 1)
                    weight_low(g * 2 + slot, slot)
            dve.wait_ge(w_hi_made, NW)
            weight_low(NW - 1, 0)

            def turn_low(i, u, k):
                src = b0[u][:, 0:D].rearrange("p (t n) -> p t n", n=N)
                dve.wait_ge(*t_hi_done.at(u, i, k))
                if k in (2, 4):
                    dve.scalar_tensor_tensor(t_lo[u][:, :, :], src, 0.0, t_hi[u][:, :, :], ALU.max, ALU.subtract)\
                       .then_inc(t_lo_done[u], 1)
                else:
                    dve.tensor_tensor(t_lo[u][:, :, :], src, t_hi[u][:, :, :], ALU.subtract).then_inc(t_lo_done[u], 1)

            def lower(i, u, w, dst, src, hi, scale):
                dve.wait_ge(*proj_hi_done.at(u, i, HI[w]))
                dve.scalar_tensor_tensor(dst, src, scale / WSCALE, hi, ALU.mult, ALU.subtract)\
                   .then_inc(proj_lo_done[u], 1)

            def across(a):
                return a[:, 0:D].rearrange("p (t n) -> p t n", n=N)

            def qkv(i, u, ws, scale):
                lower(i, u, ws[0], a_lo[u][:, :, :], across(b1[u]), a_hi[u][:, :, :], scale)
                lower(i, u, ws[1], b_lo[u][:, :, :], across(b0[u]), b_hi[u][:, :, :], 1.0)
                lower(i, u, ws[2], v_lo[u][:, :, 0:HD], s[u][:, 0, 0:D].rearrange("p (h n) -> p h n", n=HD),
                      v_hi[u][:, :, 0:HD], 1.0)

            def lessen(i, u, k, bias):
                half = k % 2
                dve.wait_ge(*scored.at(u, i, k))
                dve.tensor_tensor(score[u][:, :, :, :], s[u][:, :, 0:D].rearrange("p g (t n) -> p g t n", n=N),
                                  bias[u][:, :].unsqueeze(1).unsqueeze(1).broadcast_to([128, 2, DT, N]), ALU.add)\
                   .then_inc(biased[u], 1)
                mx = top[u][:, 2 * half:2 * half + 2, :]
                dve.wait_ge(*biased.at(u, i, k))
                dve.tensor_reduce(mx, score[u][:, :, :, :], AX.X, ALU.max).then_inc(topped[u], 1)
                if k >= 2:
                    dve.tensor_reduce(low[u][:, 2 * half:2 * half + 2, :], score[u][:, :, :, :], AX.X, ALU.min)\
                       .then_inc(lowed[u], 1)
                    dve.wait_ge(*lowed.at(u, i, k - 2))
                dve.wait_ge(*topped.at(u, i, k))
                dve.tensor_tensor(score[u][:, :, :, :], score[u][:, :, :, :],
                                  mx.unsqueeze(3).broadcast_to([128, 2, DT, N]), ALU.subtract)\
                   .then_inc(lessened[u], 1)

            def p_low(i, u, k):
                dve.wait_ge(*p_hi_done.at(u, i, k))
                dve.tensor_tensor(p_lo[u][:, :, :, :], s[u][:, :, 0:D].rearrange("p g (t n) -> p g t n", n=N),
                                  p_hi[u][:, :, :, :], ALU.subtract).then_inc(p_lo_done[u], 1)

            def attention(i, which, bias, ws, scale):
                for u in range(UNITS):
                    qkv(i, u, ws, scale)
                for half in range(2):
                    for u in range(UNITS):
                        lessen(i, u, 2 * which + half, bias)
                    for u in range(UNITS):
                        p_low(i, u, 2 * which + half)

            def divide(i, u, which):
                o = b1[u][:, 0:H * HS].rearrange("p (h c) -> p h c", c=HS)
                dve.wait_ge(*attended.at(u, i, which))
                dve.reciprocal(inv[u][:, :], o[:, :, HD]).then_inc(inverted[u], 1)
                dve.wait_ge(*inverted.at(u, i, which))
                if which == 1:
                    dve.tensor_scalar(flag[u][:, :, :], top[u][:, :, :], 0.0, None, ALU.is_equal)\
                       .then_inc(pad_step[u], 1)
                    dve.wait_ge(*pad_step.at(u, i, 0))
                    dve.wait_ge(*lowed.at(u, i, 1))
                    dve.scalar_tensor_tensor(flag[u][:, :, :], low[u][:, :, :], 0.0, flag[u][:, :, :], ALU.is_equal,
                                             ALU.mult).then_inc(pad_step[u], 1)
                    dve.wait_ge(*pad_step.at(u, i, 1))
                    dve.tensor_scalar(flag[u][:, :, :], flag[u][:, :, :], -1.0, 1.0, ALU.mult, ALU.add)\
                       .then_inc(pad_step[u], 1)
                    dve.wait_ge(*pad_step.at(u, i, 2))
                    iv = inv[u][:, :].rearrange("p (t g) -> p g t", g=HG)
                    dve.tensor_tensor(iv, iv, flag[u][:, :, :], ALU.mult).then_inc(pad_step[u], 1)
                    dve.wait_ge(*pad_step.at(u, i, 3))
                dve.tensor_tensor(z[u][:, :].rearrange("p (h c) -> p h c", c=HD), o[:, :, 0:HD],
                                  inv[u][:, :].unsqueeze(2).broadcast_to([128, H, HD]), ALU.mult)\
                   .then_inc(o_ready[u], 1)

            def moments(i, u, k, src):
                dve.bn_stats(st6[u][:, :], src).then_inc(stats_done[u], 1)
                dve.wait_ge(*stats_done.at(u, i, k))
                dve.tensor_copy(col(u, TICK), powers[:, 0:1])
                dve.bn_aggr(mv[u][:, :], st6[u][:, :]).then_inc(moments_done[u], 1)
                dve.wait_ge(*moments_done.at(u, i, k))

            def outer_begin(i, u, layer):
                k = OUTER_NORM[layer]
                moments(i, u, k, z[u][:, :])
                dve.tensor_scalar(col(u, VAR), mv[u][:, 1:2], 1e-5, None, ALU.add).then_inc(variance_done[u], 1)

            def outer_end(i, u, layer):
                if layer == 3:
                    dve.wait_ge(*stored.before(u, i))
                dve.wait_ge(*root_done.at(u, i, OUTER_NORM[layer]))
                dve.tensor_scalar((x_out if layer == 3 else x)[u][:, :], z[u][:, :], mv[u][:, 0:1], col(u, ROOT),
                                  ALU.subtract, ALU.mult).then_inc(normed[u], 1)

            def inner_end(i, u, n, bank):
                dve.scalar_tensor_tensor(zc[u], bank, mv[u][:, 0:1], rows[:, 2 * n, :], ALU.subtract, ALU.mult)\
                   .then_inc(centered[u], 1)
                dve.wait_ge(*root_done.at(u, i, INNER_NORM[n]))
                if n < 2:
                    dve.tensor_scalar(col(u, BASE), col(u, ROOT), 1e-3, col(u, DENOM), ALU.add, ALU.mult)\
                       .then_inc(gain_base[u], 1)
                    dve.wait_ge(*gain_base.at(u, i, n))
                    dve.reciprocal(col(u, GAIN), col(u, BASE)).then_inc(gain_done[u], 1)
                else:
                    dve.tensor_tensor(col(u, GAIN), col(u, ROOT), col(u, INV), ALU.mult).then_inc(gain_done[u], 1)
                dve.wait_ge(*centered.at(u, i, n))
                dve.wait_ge(*gain_done.at(u, i, n))
                dve.scalar_tensor_tensor(z[u][:, :], zc[u], col(u, GAIN), rows[:, 2 * n + 1, :], ALU.mult, ALU.add)\
                   .then_inc(inner_done[u], 1)

            dve.wait_ge(consts_made, 6)
            dve.wait_ge(small_loaded, 64)
            dve.wait_ge(dve_consts, 9)
            with dve.Fori(0, ROUNDS) as i:
                for u in range(UNITS):
                    dve.wait_ge(*adjt_done.at(u, i))
                    dve.tensor_copy(adj_t[u][:, :], s[u][:, 1, 0:N]).then_inc(masks_done[u], 1)
                    dve.tensor_scalar(mask_bias[u][:, :], adj[u][:, :], 0.0, MASKED, ALU.is_le, ALU.mult)\
                       .then_inc(masks_done[u], 1)
                    dve.wait_ge(*masks_done.at(u, i, 1))
                    dve.tensor_tensor(mask_pair[u][:, 0, :], adj_t[u][:, :], tri_temper[:, 0, :], ALU.mult)\
                       .then_inc(masks_done[u], 1)
                    dve.tensor_tensor(mask_pair[u][:, 1, :], adj[u][:, :], tri_temper[:, 1, :], ALU.mult)\
                       .then_inc(masks_done[u], 1)
                    dve.scalar_tensor_tensor(mask_bias[u][:, :], adj[u][:, :], beta[:, 0:1], mask_bias[u][:, :],
                                             ALU.mult, ALU.add).then_inc(masks_done[u], 1)
                    turn_low(i, u, 0)
                for u in range(UNITS):
                    dve.wait_ge(*masks_done.at(u, i, 4))
                attention(i, 0, mask_bias, (L0_Q, L0_K, L0_V), HD ** -0.5)
                for u in range(UNITS):
                    divide(i, u, 0)
                    dve.wait_ge(*o_ready.at(u, i, 0))
                    dve.tensor_tensor(z[u][:, :], z[u][:, :], x_in[u][:, :], ALU.add).then_inc(x_in_used[u], 1)
                    dve.wait_ge(*x_in_used.at(u, i))
                    outer_begin(i, u, 0)
                for u in range(UNITS):
                    outer_end(i, u, 0)

                for layer in range(2):
                    left, right, lin = L1_W[layer]
                    for u in range(UNITS):
                        turn_low(i, u, 1 + layer)
                    for u in range(UNITS):
                        lower(i, u, left, a_lo[u][:, :, :], across(b1[u]), a_hi[u][:, :, :], 1.0)
                        lower(i, u, right, b_lo[u][:, :, :], across(b0[u]), b_hi[u][:, :, :], 1.0)
                    for u in range(UNITS):
                        dve.wait_ge(*u_done.at(u, i, layer))
                        dve.tensor_tensor(u_pair[u][:, :, :], s[u][:, 1, 0:2 * N].rearrange("p (a n) -> p a n", n=N),
                                          mask_pair[u][:, :, :], ALU.mult).then_inc(u_masked[u], 1)
                        dve.wait_ge(*u_masked.at(u, i, layer))
                        dve.tensor_tensor(e[u][:, :], u_pair[u][:, 0, :], u_pair[u][:, 1, :], ALU.add)\
                           .then_inc(u_ready[u], 1)
                    for u in range(UNITS):
                        dve.wait_ge(*e_done.at(u, i, layer))
                        dve.tensor_tensor(delta[u][:, :], e[u][:, :], adj_t[u][:, :], ALU.mult)\
                           .then_inc(delta_done[u], 1)
                    for u in range(UNITS):
                        ctx_ = b1[u][:, 0:D]
                        dve.wait_ge(*mixed.at(u, i, layer))
                        dve.tensor_scalar(col(u, DENOM), b1[u][:, D:D + 1], 1e-10, None, ALU.add)\
                           .then_inc(denom_done[u], 1)
                        dve.wait_ge(*denom_done.at(u, i, layer))
                        dve.reciprocal(col(u, INV), col(u, DENOM)).then_inc(denom_inverted[u], 1)
                        moments(i, u, INNER_NORM[layer], ctx_)
                        dve.wait_ge(*denom_inverted.at(u, i, layer))
                        dve.tensor_scalar(col(u, INV2), col(u, INV), col(u, INV), D / (D - 1.0), ALU.mult, ALU.mult)\
                           .then_inc(inverse_squared[u], 1)
                        dve.wait_ge(*inverse_squared.at(u, i, layer))
                        dve.tensor_tensor(col(u, VAR), mv[u][:, 1:2], col(u, INV2), ALU.mult)\
                           .then_inc(variance_done[u], 1)
                        inner_end(i, u, layer, ctx_)
                for u in range(UNITS):
                    dve.wait_ge(*inner_done.at(u, i, 1))
                    dve.scalar_tensor_tensor(z[u][:, :], z[u][:, :], 0.0, x[u][:, :], ALU.max, ALU.add)\
                       .then_inc(residual_added[u], 1)
                    dve.wait_ge(*residual_added.at(u, i, 0))
                    outer_begin(i, u, 1)
                for u in range(UNITS):
                    outer_end(i, u, 1)

                for layer in range(2):
                    upper, diag, lower_w = L2_W[layer]
                    for u in range(UNITS):
                        turn_low(i, u, 3 + layer)
                    for u in range(UNITS):
                        dve.wait_ge(*u_done.at(u, i, 2 + layer))
                        dve.tensor_reduce(col(u, TOP), b1[u][:, 0:N], AX.X, ALU.max).then_inc(u_topped[u], 1)
                        dve.wait_ge(*u_topped.at(u, i, layer))
                        dve.tensor_scalar(col(u, UBIAS), col(u, TOP), -1.0 / TEMPER, None, ALU.mult)\
                           .then_inc(u_bias_ready[u], 1)
                    for u in range(UNITS):
                        dve.wait_ge(*e_done.at(u, i, 2 + layer))
                        dve.tensor_tensor_reduce(out=delta[u][:, :], in0=e[u][:, :], in1=adj[u][:, :], scale=1.0,
                                                 scalar=0.0, op0=ALU.mult, op1=ALU.add, accum_out=col(u, DSUM))\
                           .then_inc(delta_done[u], 1)
                        dve.wait_ge(*delta_done.at(u, i, 2 + layer))
                        dve.scalar_tensor_tensor(col(u, DENOM), col(u, ZSUM), 1e-10, col(u, DSUM), ALU.mult, ALU.add)\
                           .then_inc(denom_done[u], 1)
                        dve.wait_ge(*denom_done.at(u, i, 2 + layer))
                        dve.reciprocal(col(u, INV), col(u, DENOM)).then_inc(denom_inverted[u], 1)
                        dve.wait_ge(*denom_inverted.at(u, i, 2 + layer))
                        dve.tensor_tensor(col(u, INV2), col(u, INV), col(u, INV), ALU.mult)\
                           .then_inc(inverse_squared[u], 1)
                    for u in range(UNITS):
                        dve.wait_ge(*delta_turned.at(u, i, layer))
                        dve.tensor_tensor(delta3[u][:, :, :],
                                          b1[u][:, N:2 * N].unsqueeze(1).broadcast_to([128, 3, N]), tri[:, :, :],
                                          ALU.mult).then_inc(delta3_done[u], 1)
                        dve.wait_ge(*projected.at(u, i, ORDER.index(diag)))
                        dve.tensor_scalar(proj[u][:, 1, 0:D], s[u][:, 1, 0:D], 1.0 / WSCALE, None, ALU.mult)\
                           .then_inc(proj_lo_done[u], 1)
                    for u in range(UNITS):
                        ctx_ = s[u][:, 0, 0:D]
                        dve.wait_ge(*mixed.at(u, i, 2 + layer))
                        moments(i, u, INNER_NORM[2 + layer], ctx_)
                        dve.wait_ge(*inverse_squared.at(u, i, 2 + layer))
                        dve.tensor_scalar(col(u, VAR), mv[u][:, 1:2], col(u, INV2), 1e-12, ALU.mult, ALU.add)\
                           .then_inc(variance_done[u], 1)
                        inner_end(i, u, 2 + layer, ctx_)
                for u in range(UNITS):
                    dve.wait_ge(*inner_done.at(u, i, 3))
                    dve.scalar_tensor_tensor(z[u][:, :], z[u][:, :], 0.0, x[u][:, :], ALU.max, ALU.add)\
                       .then_inc(residual_added[u], 1)
                    dve.wait_ge(*residual_added.at(u, i, 1))
                    outer_begin(i, u, 2)
                for u in range(UNITS):
                    outer_end(i, u, 2)

                for u in range(UNITS):
                    turn_low(i, u, 5)
                attention(i, 1, adj, (L3_Q, L3_K, L3_V), D ** -0.5)
                for u in range(UNITS):
                    divide(i, u, 1)
                for u in range(UNITS):
                    turn_low(i, u, 6)
                for u in range(UNITS):
                    dve.wait_ge(*projected.at(u, i, ORDER.index(L3_O)))
                    dve.scalar_tensor_tensor(z[u][:, :], b1[u][:, 0:D], 1.0 / WSCALE, x[u][:, :], ALU.mult, ALU.add)\
                       .then_inc(residual_added[u], 1)
                    dve.wait_ge(*residual_added.at(u, i, 2))
                    outer_begin(i, u, 3)
                for u in range(UNITS):
                    outer_end(i, u, 3)


def kernel(**inputs):
    import numpy as _np
    import concourse.bacc as _bacc
    from concourse.bass_utils import run_bass_kernel_spmd as _run

    a = {k: _np.asarray(v) for k, v in inputs.items()}
    ws = [a["L0_gnn_Wq"], a["L0_gnn_Wk"], a["L0_gnn_Wv"]]
    for layer in range(2):
        ws += [a[f"L1_gnn_{n}"][layer].T for n in ("W_left", "W_right", "W_lin")]
    for layer in range(2):
        ws += [a[f"L2_gnn_{n}"][layer].T for n in ("Wl", "Ws", "Wr")]
    ws += [a[f"L3_gnn_{n}"].T for n in ("Wq", "Wk", "Wv", "Wo")]
    biases = [a["L0_gnn_bq"], a["L0_gnn_bk"], a["L0_gnn_bv"], a["L1_gnn_b_lin"][0], a["L1_gnn_b_lin"][1]]
    for layer in range(2):
        biases += [a[f"L2_gnn_{n}"][layer] for n in ("bl", "bs", "br")]
    biases += [a["L3_gnn_bv"], a["L3_gnn_bo"]]
    rows = []
    for layer in range(2):
        rows += [a["L1_gnn_ln_a"][layer], a["L1_gnn_ln_b"][layer]]
    for layer in range(2):
        rows += [a["L2_gnn_ln_w"][layer], a["L2_gnn_ln_b"][layer]]
    arrays = {
        "x_dram": _np.ascontiguousarray(a["x"]),
        "adj_dram": _np.ascontiguousarray(a["adj"]),
        "w_dram": _np.stack([_np.ascontiguousarray(w) for w in ws]),
        "bias_dram": _np.stack(biases),
        "rows_dram": _np.stack(rows),
        "beta_dram": a["L0_gnn_beta"].reshape(1),
    }
    nc = _bacc.Bacc("TRN2", target_bir_lowering=False, num_devices=1)
    args = [nc.dram_tensor(name, v.shape, F32, kind="ExternalInput").ap() for name, v in arrays.items()]
    out = nc.dram_tensor("out_dram", (B, N, D), F32, kind="ExternalOutput").ap()
    graph_layers(nc, *args, out)
    r = _run(nc, [arrays], core_ids=[0])
    return r.results[0]["out_dram"]
```

```python
import numpy as np
import concourse.bass as bass
from concourse import mybir
from contextlib import ExitStack

F32, F16 = mybir.dt.float32, mybir.dt.float16
ACT = mybir.ActivationFunctionType
ALU = mybir.AluOpType
AX = mybir.AxisListType

B, N, D = 64, 128, 384
H, HD = 12, 32
DT = D // 128
HG = 128 // HD
HS = HD + 1
UNITS = 4
ROUNDS = B // UNITS
assert B == UNITS * ROUNDS
WSCALE = 64.0
MASKED = -9000000000000000.0
TEMPER = float(np.sqrt(D))
BANK = 512

L0_Q, L0_K, L0_V = 0, 1, 2
L1_W = ((3, 4, 5), (6, 7, 8))
L2_W = ((9, 10, 11), (12, 13, 14))
L3_Q, L3_K, L3_V, L3_O = 15, 16, 17, 18
NW = 19
BIAS_OF = {L0_Q: 0, L0_K: 1, L0_V: 2, 5: 3, 8: 4, 9: 5, 10: 6, 11: 7, 12: 8, 13: 9, 14: 10, L3_V: 11, L3_O: 12}
NB = 13
NR = 8


PE, SCALAR, VECTOR, POOL, SYNC = "PE", "SCALAR", "VECTOR", "POOL", "SYNC"
PERIOD = UNITS * 64.00
TIMES = {
    ("turn", 0): {PE: 0.0, SCALAR: 0.6, VECTOR: 1.3},
    ("masks", 0): {PE: 0.3, VECTOR: 1.8},
    ("project", 2): {PE: 2.2, SCALAR: 4.1, VECTOR: 5.9},
    ("project", 0): {PE: 3.8, SCALAR: 6.0, VECTOR: 6.9},
    ("project", 1): {PE: 6.7, SCALAR: 8.7, VECTOR: 9.3},
    ("scores", 0): {PE: 10.5, VECTOR: 11.8, SCALAR: 14.0},
    ("turn_p", 0): {PE: 17.1, SCALAR: 18.1, VECTOR: 19.1},
    ("attend", 0): {PE: 20.2},
    ("divide", 0): {VECTOR: 21.1},
    ("scores", 1): {PE: 21.9, VECTOR: 23.2, SCALAR: 25.4},
    ("turn_p", 1): {PE: 28.1, SCALAR: 29.1, VECTOR: 30.7},
    ("attend", 1): {PE: 31.8},
    ("divide", 1): {VECTOR: 32.6},
    ("residual", 0): {VECTOR: 33.1, POOL: 35.0},
    ("norm", 0): {VECTOR: 35.7},
    ("turn", 1): {PE: 36.3, SCALAR: 36.9, VECTOR: 37.5},
    ("project", 3): {PE: 38.3, SCALAR: 40.1, VECTOR: 42.0},
    ("project", 4): {PE: 39.8, SCALAR: 41.7, VECTOR: 42.5},
    ("u_gcn", 0): {PE: 43.2, VECTOR: 44.5, SCALAR: 45.5},
    ("project", 5): {PE: 44.2, SCALAR: 46.3},
    ("delta_gcn", 0): {VECTOR: 46.1},
    ("mix", 0): {PE: 46.9},
    ("inner", 0): {VECTOR: 47.9, POOL: 49.9},
    ("gain", 0): {VECTOR: 50.5},
    ("turn", 2): {PE: 52.0, SCALAR: 52.7, VECTOR: 53.5},
    ("project", 6): {PE: 54.2, SCALAR: 57.3, VECTOR: 58.3},
    ("project", 7): {PE: 55.8, SCALAR: 57.7, VECTOR: 58.8},
    ("u_gcn", 1): {PE: 61.2, VECTOR: 62.5, SCALAR: 63.5},
    ("project", 8): {PE: 62.2, SCALAR: 65.0},
    ("delta_gcn", 1): {VECTOR: 64.1},
    ("mix", 1): {PE: 69.5},
    ("inner", 1): {VECTOR: 71.4, POOL: 73.5},
    ("gain", 1): {VECTOR: 74.0},
    ("residual", 1): {VECTOR: 77.7, POOL: 80.0},
    ("norm", 1): {VECTOR: 80.6},
    ("turn", 3): {PE: 81.8, SCALAR: 82.8, VECTOR: 83.9},
    ("u_di", 0): {PE: 84.8, VECTOR: 86.2, SCALAR: 87.2},
    ("project", 9): {PE: 87.0, SCALAR: 91.6},
    ("delta_di", 0): {VECTOR: 89.1},
    ("project", 10): {PE: 90.1, SCALAR: 92.1},
    ("project", 11): {PE: 92.8, SCALAR: 96.5},
    ("turn_delta", 0): {PE: 94.5, VECTOR: 95.5},
    ("mix", 2): {PE: 97.4},
    ("inner", 2): {VECTOR: 100.0, POOL: 102.3},
    ("gain", 2): {VECTOR: 102.8},
    ("turn", 4): {PE: 105.4, SCALAR: 106.0, VECTOR: 109.2},
    ("u_di", 1): {PE: 109.9, VECTOR: 110.7, SCALAR: 111.4},
    ("project", 12): {PE: 111.6, SCALAR: 113.5},
    ("project", 13): {PE: 113.2, SCALAR: 115.7},
    ("delta_di", 1): {VECTOR: 113.7},
    ("project", 14): {PE: 116.3, SCALAR: 118.3},
    ("turn_delta", 1): {PE: 118.0, VECTOR: 118.4},
    ("mix", 3): {PE: 121.3},
    ("inner", 3): {VECTOR: 124.2, POOL: 126.1},
    ("gain", 3): {VECTOR: 127.1},
    ("residual", 2): {VECTOR: 131.1, POOL: 133.1},
    ("norm", 2): {VECTOR: 134.4},
    ("turn", 5): {PE: 136.4, SCALAR: 137.0, VECTOR: 138.8},
    ("project", 17): {PE: 139.8, SCALAR: 143.8, VECTOR: 144.9},
    ("project", 15): {PE: 141.4, SCALAR: 147.1, VECTOR: 150.6},
    ("project", 16): {PE: 146.2, SCALAR: 148.0, VECTOR: 149.6},
    ("scores", 2): {PE: 152.6, VECTOR: 154.4, SCALAR: 157.8},
    ("turn_p", 2): {PE: 160.3, SCALAR: 161.8, VECTOR: 162.7},
    ("attend", 2): {PE: 164.6},
    ("divide", 2): {VECTOR: 167.5},
    ("scores", 3): {PE: 169.7, VECTOR: 182.9, SCALAR: 186.2},
    ("turn_p", 3): {PE: 188.3, SCALAR: 189.4, VECTOR: 192.3},
    ("attend", 3): {PE: 193.4},
    ("divide", 3): {VECTOR: 196.7},
    ("turn", 6): {PE: 200.7, SCALAR: 201.4, VECTOR: 203.3},
    ("project", 18): {PE: 207.0},
    ("residual", 3): {VECTOR: 209.4, POOL: 211.2},
    ("norm", 3): {VECTOR: 212.4},
}
TIMES[("store", 0)] = {SYNC: TIMES[("norm", 3)][VECTOR] + 0.3}
TIMES[("load", 0)] = {SYNC: 0.0}


def steps_of(engine, *names):
    return sorted((s for s in TIMES if engine in TIMES[s] and (not names or s[0] in names)),
                  key=lambda s: TIMES[s][engine])


def body(engine):
    at = []
    for u in range(UNITS):
        for step in steps_of(engine):
            t = TIMES[step][engine] + PERIOD * u / UNITS
            at.append((t % PERIOD, *step, u, int(t >= PERIOD)))
    return [x[1:] for x in sorted(at)]


class Signal:

    def __init__(self, ctx, nc, name, per_round=1, step=1, primed=0):
        self.sems = [ctx.enter_context(nc.semaphore(f"{name}_{u}")) for u in range(UNITS)]
        self.per_round, self.step, self.primed = per_round, step, primed

    def prime(self, eng):
        assert self.primed == 1
        for sem in self.sems:
            eng.sem_inc(sem, 1)

    def __getitem__(self, u):
        return self.sems[u]

    def at(self, u, i, k=0):
        return self.sems[u], i * (self.per_round * self.step) + ((k + 1) * self.step + self.primed)

    def before(self, u, i):
        assert self.primed == 1
        return self.sems[u], i * (self.per_round * self.step) + 1


def graph_layers(nc, x_d, adj_d, w_d, bias_d, rows_d, beta_d, out_d):
    ctx = ExitStack()
    with ctx:
        def sb(name, shape, dt=F32):
            return ctx.enter_context(nc.sbuf_tensor(name, shape, dt))

        def per_unit(name, shape, dt=F32):
            return [sb(f"{name}_{u}", shape, dt) for u in range(UNITS)]

        def sem(name):
            return ctx.enter_context(nc.semaphore(name))

        def signal(name, per_round=1, step=1, primed=0):
            return Signal(ctx, nc, name, per_round, step, primed)

        w_hi = sb("w_hi", [128, NW, DT, D], F16)
        w_lo = sb("w_lo", [128, NW, DT, D], F16)
        bias_rows = sb("bias_rows", [128, NB, D], F16)
        ones = sb("ones", [128, 128], F16)
        rows = sb("rows", [128, NR, D])
        ident = sb("ident", [128, 128])
        tri = sb("tri", [128, 3, 128])
        tri_temper = sb("tri_temper", [128, 2, 128])
        beta = sb("beta", [128, 1])
        powers = sb("powers", [128, 2])

        adj = per_unit("adj", [128, N])
        adj_t = per_unit("adj_t", [128, N])
        mask_bias = per_unit("mask_bias", [128, N])
        mask_pair = per_unit("mask_pair", [128, 2, N])
        x = per_unit("x", [128, D])
        z = per_unit("z", [128, D])
        t_hi = per_unit("t_hi", [128, DT, N], F16)
        t_lo = per_unit("t_lo", [128, DT, N], F16)
        v_hi = per_unit("v_hi", [128, H, HS], F16)
        v_lo = per_unit("v_lo", [128, H, HS], F16)
        top = per_unit("top", [128, HG, DT])
        low = per_unit("low", [128, HG, DT])
        inv = per_unit("inv", [128, HG, DT])
        flag = per_unit("flag", [128, HG, DT])
        u_pair = per_unit("u_pair", [128, 2, N])
        e = per_unit("e", [128, N])
        delta = per_unit("delta", [128, N])
        st6 = per_unit("st6", [128, 6])
        mv = per_unit("mv", [128, 2])
        small = per_unit("small", [128, 12])
        VAR, ROOT, DENOM, INV, INV2, BASE, GAIN, TOP, UBIAS, ZSUM, DSUM, TICK = range(12)

        def col(u, c):
            return small[u][:, c:c + 1]

        AB = DT * N // 2
        ab = sb("ab", [128, UNITS * 4 * AB])
        w_stage = ab[:, 0:2 * DT * D].rearrange("p (s t o) -> p s t o", s=2, t=DT)
        a_hi, a_lo, b_hi, b_lo = (
            [ab[:, (4 * u + n) * AB:(4 * u + n + 1) * AB].bitcast(F16).rearrange("p (t n) -> p t n", n=N)
             for u in range(UNITS)] for n in range(4))
        SCORES, PROJ = 2 * DT * N, 3 * (D + 1)
        shared = sb("shared", [128, UNITS * (SCORES + PROJ)])
        scores_at = [shared[:, u * SCORES:(u + 1) * SCORES] for u in range(UNITS)]
        proj_at = [shared[:, UNITS * SCORES + u * PROJ:UNITS * SCORES + (u + 1) * PROJ] for u in range(UNITS)]
        score = [a.rearrange("p (g t n) -> p g t n", g=2, t=DT) for a in scores_at]
        delta3 = [a[:, 0:3 * N].rearrange("p (m n) -> p m n", m=3) for a in scores_at]
        zc = [a[:, 3 * N:3 * N + D] for a in scores_at]
        out = zc
        proj = [a.rearrange("p (m d) -> p m d", m=3) for a in proj_at]
        p_hi, p_lo = ([a[:, D + 1 + n * DT * N:D + 1 + (n + 1) * DT * N].bitcast(F16)
                        .rearrange("p (g t n) -> p g t n", g=2, t=DT) for a in proj_at] for n in range(2))
        bias_stage = shared[:, 0:NB * D].rearrange("p (b d) -> p b d", d=D)

        banks = [ctx.enter_context(nc.psum_tensor(f"banks_{u}", [128, 2, BANK], F32)) for u in range(UNITS)]
        b0 = [a[:, 0, :] for a in banks]
        b1 = [a[:, 1, :] for a in banks]
        blocks = [a[:, :, 0:D].rearrange("p g (t n) -> p g t n", n=N) for a in banks]

        w_loaded = [sem("w_loaded_even"), sem("w_loaded_odd")]
        w_hi_made, w_lo_made = sem("w_hi_made"), sem("w_lo_made")
        small_loaded = sem("small_loaded")
        consts_cleared, consts_made = sem("consts_cleared"), sem("consts_made")
        dve_consts = sem("dve_consts")
        bias_hi_made, bias_made = sem("bias_hi_made"), sem("bias_made")
        rows_loaded, bias_rows_cleared = sem("rows_loaded"), sem("bias_rows_cleared")
        loaded = signal("loaded", step=32)
        stored = signal("stored", step=16, primed=1)
        TURNED = steps_of(PE, "masks", "turn", "turn_delta")
        turned = signal("turned", len(TURNED))
        projected = signal("projected", NW)
        scored = signal("scored", 4)
        p_turned = signal("p_turned", 4)
        attended = signal("attended", 4)
        u_done = signal("u_done", 4)
        mixed = signal("mixed", 4)
        t_hi_done = signal("t_hi_done", 7)
        proj_hi_done = signal("proj_hi_done", 18)
        exp_done = signal("exp_done", 4)
        p_hi_done = signal("p_hi_done", 4)
        e_done = signal("e_done", 4)
        masks_done = signal("masks_done", 5)
        t_lo_done = signal("t_lo_done", 7)
        proj_lo_done = signal("proj_lo_done", 10)
        biased = signal("biased", 4)
        topped = signal("topped", 4)
        p_lo_done = signal("p_lo_done", 4)
        o_ready = signal("o_ready", 4)
        residual_added = signal("residual_added", 4, primed=1)
        u_ready = signal("u_ready", 2)
        u_bias_ready = signal("u_bias_ready", 2)
        delta_done = signal("delta_done", 4)
        delta3_done = signal("delta3_done", 2)
        MOMENTS = steps_of(VECTOR, "inner", "residual")
        moments_done = signal("moments_done", 2 * 8)
        variance_done = signal("variance_done", 8)
        inner_done = signal("inner_done", 4)
        normed = signal("normed", 4)
        NUMBERS = []
        for name_, k_ in steps_of(VECTOR):
            NUMBERS += [(what, k_) for what in {
                "scores": ("minimum",) if k_ >= 2 else (),
                "divide": ("inverse",) if k_ < 2 else ("inverse", "top is 0", "row is 0", "row is not 0", "kept"),
                "u_gcn": ("masked",), "u_di": ("top of u",),
                "delta_di": ("sum 2", "inverse sum 2", "inverse squared 2"),
                "inner": ("sum", "inverse sum", "inverse squared", "centred") if k_ < 2 else ("centred",),
                "gain": ("gain base", "gain") if k_ < 2 else ("gain",)}.get(name_, ())]
        numbers = signal("numbers", len(NUMBERS))
        root_done = signal("root_done", 8)
        ROOTS = steps_of(POOL)

        ORDER = {w: n for n, (_, w) in enumerate(steps_of(PE, "project"))}
        HI = {w: n for n, (_, w) in enumerate(steps_of(SCALAR, "project"))}
        LO = {w: n for n, (_, w) in enumerate(steps_of(VECTOR, "project"))}

        def number(u, r, what, k):
            return numbers.at(u, r, NUMBERS.index((what, k)))

        def exponent(name, k):
            return powers[:, 0:1] if name == "inner" and k < 2 else powers[:, 1:2]

        def rounds(eng, engine, take):
            order = body(engine)
            for name, k, u, back in order:
                if not back:
                    take(name, k, 0, u)
            with eng.Fori(1, ROUNDS) as i:
                for n, (name, k, u, back) in enumerate(order):
                    if n % 8 == 0:
                        now = nc.snap(i, engines=[eng.engine])
                    take(name, k, now - back, u)
            for name, k, u, back in order:
                if back:
                    take(name, k, ROUNDS - 1, u)

        block = ctx.enter_context(nc.Block())

        DVE_CONSTS = 3 + 3 * UNITS

        ACROSS = (L0_Q, L0_K, *L1_W[0][:2], *L1_W[1][:2], L3_Q, L3_K)
        TURN_OF = {L0_Q: 0, L0_K: 0, L0_V: 0, **{w: 1 + n for n in range(2) for w in L1_W[n]},
                   **{w: 3 + n for n in range(2) for w in L2_W[n]}, L3_Q: 5, L3_K: 5, L3_V: 5, L3_O: 6}

        def across(bank):
            return bank[:, 0:D].rearrange("p (t n) -> p t n", n=N)

        def bank_of(u, w):
            in_b1 = (L0_Q, L1_W[0][0], L1_W[1][0], L2_W[0][1], L2_W[1][1], L3_Q, L3_O)
            return (b1 if w in in_b1 else b0)[u]

        def place_of(u, w):
            bank = bank_of(u, w)
            if w in ACROSS:
                scale = {L0_Q: HD ** -0.5, L3_Q: D ** -0.5}.get(w, 1.0)
                return (a_hi if bank is b1[u] else b_hi)[u], across(bank), scale
            if w in (L0_V, L3_V):
                return v_hi[u][:, :, 0:HD], bank[:, 0:D].rearrange("p (h n) -> p h n", n=HD), 1.0
            m = 0 if w in (L1_W[0][2], L1_W[1][2]) else (w - L2_W[0][0]) % 3
            return proj[u][:, m, 0:D], bank[:, 0:D], 1.0

        def low_of(u, w):
            if w in ACROSS:
                return (a_lo if bank_of(u, w) is b1[u] else b_lo)[u]
            return v_lo[u][:, :, 0:HD]

        @block.sync
        def _(sp):
            stored.prime(sp)

            def load_weight(w, slot):
                sp.dma_start(w_stage[:, slot, :, :], w_d[w].rearrange("(t p) o -> p t o", p=128)).then_inc(w_loaded[slot], 16)

            sp.dma_start(beta[:, :], beta_d.partition_broadcast(128)).then_inc(small_loaded, 16)
            for row in (0, 32):
                sp.dma_start(bias_stage[row:row + 1, :, :], bias_d.rearrange("(a b) d -> a b d", a=1))\
                  .then_inc(small_loaded, 16)
            load_weight(0, 0)
            load_weight(1, 1)
            sp.dma_start(rows[:, :, :], rows_d.rearrange("r d -> (r d)").partition_broadcast(128)
                         .rearrange("p (r d) -> p r d", d=D)).then_inc(rows_loaded, 16)

            def load(r, u):
                sp.dma_start(x[u][:, :], x_d[r * UNITS + u]).then_inc(loaded[u], 16)
                sp.dma_start(adj[u][:, :], adj_d[r * UNITS + u]).then_inc(loaded[u], 16)

            for u in range(UNITS):
                load(0, u)
            with sp.Fori(1, NW // 2) as g:
                for slot in range(2):
                    sp.wait_ge(w_lo_made, g * 2 + slot - 1)
                    load_weight(g * 2 + slot, slot)
            sp.wait_ge(w_lo_made, NW - 2)
            load_weight(NW - 1, 0)

            def take(name, k, r, u):
                if name == "load" and not isinstance(r, int):
                    sp.wait_ge(*residual_added.before(u, r))
                    load(r, u)
                if name == "store":
                    sp.wait_ge(*normed.at(u, r, 3))
                    sp.dma_start(out_d[r * UNITS + u], out[u]).then_inc(stored[u], 16)

            rounds(sp, SYNC, take)
            for u in range(UNITS):
                sp.wait_ge(*stored.before(u, ROUNDS))

        @block.gpsimd
        def _(pool):
            pool.memset(bias_rows[:, :, :], 0.0).then_inc(bias_rows_cleared, 1)
            pool.memset(ident[:, :], 0.0).then_inc(consts_cleared, 1)
            pool.memset(tri[:, :, :], 1.0).then_inc(consts_cleared, 1)
            pool.memset(tri_temper[:, :, :], 1.0 / TEMPER).then_inc(consts_cleared, 1)
            pool.wait_ge(consts_cleared, 3)
            pool.affine_select(out=ident[:, :], in_=ident[:, :], compare_op=ALU.not_equal, fill=1.0, base=0,
                               pattern=[[-1, 128]], channel_multiplier=1).then_inc(consts_made, 1)
            for m, op, sign in ((0, ALU.is_gt, 1), (1, ALU.is_equal, 1), (2, ALU.is_gt, -1)):
                pool.affine_select(out=tri[:, m, :], in_=tri[:, m, :], compare_op=op, fill=0.0, base=0,
                                   pattern=[[-sign, 128]], channel_multiplier=sign).then_inc(consts_made, 1)
            for m, op, sign in ((0, ALU.is_ge, 1), (1, ALU.is_gt, -1)):
                pool.affine_select(out=tri_temper[:, m, :], in_=tri_temper[:, m, :], compare_op=op, fill=0.0, base=0,
                                   pattern=[[-sign, 128]], channel_multiplier=sign).then_inc(consts_made, 1)
            pool.wait_ge(dve_consts, 2)

            def take(name, k, r, u):
                pool.wait_ge(*variance_done.at(u, r, MOMENTS.index((name, k))))
                pool.tensor_tensor(col(u, ROOT), col(u, VAR), exponent(name, k), ALU.pow).then_inc(root_done[u], 1)

            rounds(pool, POOL, take)

        @block.scalar
        def _(act):
            act.wait_ge(small_loaded, 48)
            act.wait_ge(bias_rows_cleared, 1)
            for row in (0, 32):
                act.activation(bias_rows[row:row + 1, :, :], bias_stage[row:row + 1, :, :], ACT.Copy, scale=WSCALE)\
                   .then_inc(bias_hi_made, 1)

            def weight_high(w, slot):
                act.activation(w_hi[:, bass.ds(w, 1), :, :].rearrange("p a t o -> p (a t o)"),
                               w_stage[:, slot, :, :].rearrange("p t o -> p (t o)"), ACT.Copy, scale=WSCALE)\
                   .then_inc(w_hi_made, 1)

            with act.Fori(0, NW // 2) as g:
                for slot in range(2):
                    act.wait_ge(w_loaded[slot], g * 16 + 16)
                    weight_high(g * 2 + slot, slot)
            act.wait_ge(w_loaded[0], 16 * (NW // 2) + 16)
            weight_high(NW - 1, 0)
            act.wait_ge(w_lo_made, NW)
            act.wait_ge(bias_made, 1)

            def turn(r, u, k):
                act.wait_ge(*turned.at(u, r, TURNED.index(("turn", k))))
                act.activation(t_hi[u][:, :, :], across(b0[u]), ACT.Relu if k in (2, 4) else ACT.Copy)\
                   .then_inc(t_hi_done[u], 1)

            def project(r, u, w):
                act.wait_ge(*projected.at(u, r, ORDER[w]))
                dst, src, scale = place_of(u, w)
                act.activation(dst, src, ACT.Copy, scale=scale / WSCALE).then_inc(proj_hi_done[u], 1)

            def scores(r, u, k):
                act.wait_ge(*topped.at(u, r, k))
                for g2 in range(2):
                    for t in range(DT):
                        last = act.activation(score[u][:, g2, t, :], score[u][:, g2, t, :], ACT.Exp,
                                              bias=top[u][:, 2 * (k % 2) + g2, t:t + 1])
                last.then_inc(exp_done[u], 1)

            def turn_p(r, u, k):
                act.wait_ge(*p_turned.at(u, r, k))
                act.activation(p_hi[u], blocks[u], ACT.Copy).then_inc(p_hi_done[u], 1)

            def u_gcn(r, u, layer):
                act.wait_ge(*u_ready.at(u, r, layer))
                act.activation(e[u][:, :], e[u][:, :], ACT.Exp).then_inc(e_done[u], 1)

            def u_di(r, u, layer):
                act.wait_ge(*u_bias_ready.at(u, r, layer))
                act.activation(e[u][:, :], b1[u][:, 0:N], ACT.Exp, bias=col(u, UBIAS), scale=1.0 / TEMPER,
                               accum_out=col(u, ZSUM)).then_inc(e_done[u], 1)

            def take(name, k, r, u):
                {"turn": turn, "project": project, "scores": scores, "turn_p": turn_p, "u_gcn": u_gcn,
                 "u_di": u_di}[name](r, u, k)

            rounds(act, SCALAR, take)

        @block.tensor
        def _(pe):
            def transpose_tiles(u, src):
                for t in range(DT):
                    last = pe.transpose(b0[u][:, t * N:(t + 1) * N], src[:, t * 128:(t + 1) * 128], ident[:, :])
                return last

            def masks(r, u, k):
                pe.wait_ge(*loaded.at(u, r))
                pe.wait_ge(*residual_added.before(u, r))
                pe.transpose(b1[u][:, 0:N], adj[u][:, :], ident[:, :]).then_inc(turned[u], 1)

            def turn(r, u, k):
                if k == 0:
                    pe.wait_ge(*loaded.at(u, r))
                    pe.wait_ge(*residual_added.before(u, r))
                    src = x
                elif k in (2, 4):
                    pe.wait_ge(*inner_done.at(u, r, k - 2))
                    src = z
                elif k in (1, 3, 5):
                    pe.wait_ge(*normed.at(u, r, k // 2))
                    src = x
                else:
                    pe.wait_ge(*o_ready.at(u, r, 3))
                    src = z
                transpose_tiles(u, src[u]).then_inc(turned[u], 1)

            def project_across(u, w, out):
                for t in range(DT):
                    o = out[:, t * N:(t + 1) * N]
                    cols = slice(t * 128, (t + 1) * 128)
                    for k in range(DT):
                        pe.matmul(o, lhsT=w_hi[:, w, k, cols], rhs=t_hi[u][:, k, :], start=(k == 0), stop=False)
                        pe.matmul(o, lhsT=w_hi[:, w, k, cols], rhs=t_lo[u][:, k, :], start=False, stop=False)
                        last = pe.matmul(o, lhsT=w_lo[:, w, k, cols], rhs=t_hi[u][:, k, :], start=False,
                                         stop=(k == DT - 1 and w not in BIAS_OF))
                    if w in BIAS_OF:
                        last = pe.matmul(o, lhsT=bias_rows[:, BIAS_OF[w], cols], rhs=ones[:, :], start=False, stop=True)
                last.then_inc(projected[u], 1)

            def project_natural(u, w, out):
                for k in range(DT):
                    pe.matmul(out, lhsT=t_hi[u][:, k, :], rhs=w_hi[:, w, k, :], start=(k == 0), stop=False)
                    pe.matmul(out, lhsT=t_hi[u][:, k, :], rhs=w_lo[:, w, k, :], start=False, stop=False)
                    pe.matmul(out, lhsT=t_lo[u][:, k, :], rhs=w_hi[:, w, k, :], start=False, stop=False)
                pe.matmul(out, lhsT=ones[:, :], rhs=bias_rows[:, BIAS_OF[w], :], start=False, stop=True)\
                  .then_inc(projected[u], 1)

            def project(r, u, w):
                pe.wait_ge(*t_lo_done.at(u, r, TURN_OF[w]))
                if w == L0_Q:
                    pe.wait_ge(*masks_done.at(u, r, 0))
                if w in (L0_K, L3_K):
                    pe.wait_ge(*proj_lo_done.at(u, r, LO[w + 1]))
                if w in (L1_W[0][2], L1_W[1][2]):
                    pe.wait_ge(*proj_lo_done.at(u, r, LO[w - 1]))
                if w in (L2_W[0][1], L2_W[1][1]):
                    pe.wait_ge(*e_done.at(u, r, 2 + (w == L2_W[1][1])))
                if w in (L2_W[0][2], L2_W[1][2]):
                    pe.wait_ge(*proj_hi_done.at(u, r, HI[w - 2]))
                if w in ACROSS:
                    project_across(u, w, bank_of(u, w))
                else:
                    project_natural(u, w, bank_of(u, w)[:, 0:D])

            def product(out, ahi, alo, bhi, blo):
                for k in range(DT):
                    pe.matmul(out, lhsT=ahi[:, k, :], rhs=bhi[:, k, :], start=(k == 0), stop=False)
                    pe.matmul(out, lhsT=ahi[:, k, :], rhs=blo[:, k, :], start=False, stop=False)
                    last = pe.matmul(out, lhsT=alo[:, k, :], rhs=bhi[:, k, :], start=False, stop=(k == DT - 1))
                return last

            def scores(r, u, k):
                pe.wait_ge(*proj_lo_done.at(u, r, max(LO[w] for w in ((L0_Q, L0_K, L0_V) if k < 2 else
                                                                      (L3_Q, L3_K, L3_V)))))
                if k % 2:
                    pe.wait_ge(*o_ready.at(u, r, k - 1))
                for t in range(DT):
                    for qp, kp, n in ((a_hi, b_hi, 0), (a_hi, b_lo, 1), (a_lo, b_hi, 2)):
                        for g2 in range(2):
                            rows_ = slice(HD * (2 * (k % 2) + g2), HD * (2 * (k % 2) + g2) + HD)
                            last = pe.matmul(banks[u][:, g2, t * N:(t + 1) * N], lhsT=qp[u][rows_, t, :],
                                             rhs=kp[u][rows_, t, :], start=(n == 0), stop=(n == 2))
                last.then_inc(scored[u], 1)

            def turn_p(r, u, k):
                pe.wait_ge(*exp_done.at(u, r, k))
                for g2 in range(2):
                    for t in range(DT):
                        last = pe.transpose(banks[u][:, g2, t * N:(t + 1) * N], score[u][:, g2, t, :], ident[:, :])
                last.then_inc(p_turned[u], 1)

            def attend(r, u, k):
                pe.wait_ge(*p_lo_done.at(u, r, k))
                for g2 in range(2):
                    for t in range(DT):
                        h = HG * t + 2 * (k % 2) + g2
                        o = b0[u][:, (DT * g2 + t) * HS:(DT * g2 + t + 1) * HS]
                        pe.matmul(o, lhsT=p_hi[u][:, g2, t, :], rhs=v_hi[u][:, h, :], start=True, stop=False)
                        pe.matmul(o, lhsT=p_hi[u][:, g2, t, :], rhs=v_lo[u][:, h, :], start=False, stop=False)
                        last = pe.matmul(o, lhsT=p_lo[u][:, g2, t, :], rhs=v_hi[u][:, h, :], start=False, stop=True)
                last.then_inc(attended[u], 1)

            def u_gcn(r, u, layer):
                pe.wait_ge(*proj_lo_done.at(u, r, max(LO[w] for w in L1_W[layer][:2])))
                product(b1[u][:, 0:N], a_hi[u], a_lo[u], t_hi[u], t_lo[u])
                product(b1[u][:, N:2 * N], b_hi[u], b_lo[u], t_hi[u], t_lo[u]).then_inc(u_done[u], 1)

            def u_di(r, u, layer):
                pe.wait_ge(*t_lo_done.at(u, r, 3 + layer))
                product(b1[u][:, 0:N], t_hi[u], t_lo[u], t_hi[u], t_lo[u]).then_inc(u_done[u], 1)

            def turn_delta(r, u, layer):
                pe.wait_ge(*delta_done.at(u, r, 2 + layer))
                pe.wait_ge(*proj_hi_done.at(u, r, HI[L2_W[layer][1]]))
                pe.transpose(b1[u][:, 0:N], delta[u][:, :], ident[:, :]).then_inc(turned[u], 1)

            def mix(r, u, k):
                if k < 2:
                    pe.wait_ge(*proj_hi_done.at(u, r, HI[L1_W[k][2]]))
                    pe.wait_ge(*delta_done.at(u, r, k))
                    pe.matmul(b1[u][:, 0:D + 1], lhsT=delta[u][:, :], rhs=proj[u][:, 0, :], start=True, stop=True)\
                      .then_inc(mixed[u], 1)
                else:
                    pe.wait_ge(*proj_hi_done.at(u, r, max(HI[w] for w in L2_W[k - 2])))
                    pe.wait_ge(*delta3_done.at(u, r, k - 2))
                    for m in range(3):
                        last = pe.matmul(b0[u][:, 0:D], lhsT=delta3[u][:, m, :], rhs=proj[u][:, m, 0:D],
                                         start=(m == 0), stop=(m == 2))
                    last.then_inc(mixed[u], 1)

            pe.wait_ge(w_lo_made, NW)
            pe.wait_ge(bias_made, 1)
            pe.wait_ge(consts_made, 6)
            pe.wait_ge(dve_consts, DVE_CONSTS)

            def take(name, k, r, u):
                {"masks": masks, "turn": turn, "project": project, "scores": scores, "turn_p": turn_p,
                 "attend": attend, "u_gcn": u_gcn, "u_di": u_di, "turn_delta": turn_delta, "mix": mix}[name](r, u, k)

            rounds(pe, PE, take)

        @block.vector
        def _(dve):
            residual_added.prime(dve)
            dve.memset(powers[:, 0:1], 0.5).then_inc(dve_consts, 1)
            dve.memset(powers[:, 1:2], -0.5).then_inc(dve_consts, 1)
            dve.memset(ones[:, :], 1.0).then_inc(dve_consts, 1)
            for u in range(UNITS):
                dve.memset(v_hi[u][:, :, HD:HS], 1.0).then_inc(dve_consts, 1)
                dve.memset(v_lo[u][:, :, HD:HS], 0.0).then_inc(dve_consts, 1)
            dve.wait_ge(bias_hi_made, 2)
            dve.scalar_tensor_tensor(bias_rows[32:33, :, :], bias_stage[32:33, :, :], WSCALE, bias_rows[32:33, :, :],
                                     ALU.mult, ALU.subtract).then_inc(bias_made, 1)
            dve.wait_ge(bias_made, 1)
            for u in range(UNITS):
                dve.memset(proj[u][:, 0, D:D + 1], 1.0).then_inc(dve_consts, 1)

            def weight_low(w, slot):
                at = bass.ds(w, 1)
                dve.scalar_tensor_tensor(w_lo[:, at, :, :].rearrange("p a t o -> p (a t o)"),
                                         w_stage[:, slot, :, :].rearrange("p t o -> p (t o)"), WSCALE,
                                         w_hi[:, at, :, :].rearrange("p a t o -> p (a t o)"),
                                         ALU.mult, ALU.subtract).then_inc(w_lo_made, 1)

            with dve.Fori(0, NW // 2) as g:
                for slot in range(2):
                    dve.wait_ge(w_hi_made, g * 2 + slot + 1)
                    weight_low(g * 2 + slot, slot)
            dve.wait_ge(w_hi_made, NW)
            weight_low(NW - 1, 0)

            def masks(r, u, k):
                dve.wait_ge(*turned.at(u, r, TURNED.index(("masks", 0))))
                dve.tensor_copy(adj_t[u][:, :], b1[u][:, 0:N]).then_inc(masks_done[u], 1)
                dve.tensor_scalar(mask_bias[u][:, :], adj[u][:, :], 0.0, MASKED, ALU.is_le, ALU.mult)\
                   .then_inc(masks_done[u], 1)
                dve.wait_ge(*masks_done.at(u, r, 1))
                dve.tensor_tensor(mask_pair[u][:, 0, :], adj_t[u][:, :], tri_temper[:, 0, :], ALU.mult)\
                   .then_inc(masks_done[u], 1)
                dve.tensor_tensor(mask_pair[u][:, 1, :], adj[u][:, :], tri_temper[:, 1, :], ALU.mult)\
                   .then_inc(masks_done[u], 1)
                dve.scalar_tensor_tensor(mask_bias[u][:, :], adj[u][:, :], beta[:, 0:1], mask_bias[u][:, :],
                                         ALU.mult, ALU.add).then_inc(masks_done[u], 1)

            def turn(r, u, k):
                dve.wait_ge(*t_hi_done.at(u, r, k))
                if k in (2, 4):
                    dve.scalar_tensor_tensor(t_lo[u][:, :, :], across(b0[u]), 0.0, t_hi[u][:, :, :], ALU.max,
                                             ALU.subtract).then_inc(t_lo_done[u], 1)
                else:
                    dve.tensor_tensor(t_lo[u][:, :, :], across(b0[u]), t_hi[u][:, :, :], ALU.subtract)\
                       .then_inc(t_lo_done[u], 1)

            def project(r, u, w):
                dve.wait_ge(*proj_hi_done.at(u, r, HI[w]))
                hi, src, scale = place_of(u, w)
                lo = low_of(u, w)
                dve.scalar_tensor_tensor(lo, src, scale / WSCALE, hi, ALU.mult, ALU.subtract)\
                   .then_inc(proj_lo_done[u], 1)

            def scores(r, u, k):
                if k == 0:
                    dve.wait_ge(*masks_done.at(u, r, 4))
                    dve.wait_ge(*stored.before(u, r))
                dve.wait_ge(*scored.at(u, r, k))
                dve.tensor_tensor(score[u], blocks[u], (mask_bias if k < 2 else adj)[u][:, :].unsqueeze(1).unsqueeze(1)
                                  .broadcast_to([128, 2, DT, N]), ALU.add).then_inc(biased[u], 1)
                heads = slice(2 * (k % 2), 2 * (k % 2) + 2)
                dve.wait_ge(*biased.at(u, r, k))
                if k >= 2:
                    dve.tensor_reduce(low[u][:, heads, :], score[u], AX.X, ALU.min).then_inc(numbers[u], 1)
                    dve.wait_ge(*number(u, r, "minimum", k))
                dve.tensor_reduce(top[u][:, heads, :], score[u], AX.X, ALU.max, negate=True).then_inc(topped[u], 1)

            def turn_p(r, u, k):
                dve.wait_ge(*p_hi_done.at(u, r, k))
                dve.tensor_tensor(p_lo[u], blocks[u], p_hi[u], ALU.subtract).then_inc(p_lo_done[u], 1)

            def divide(r, u, k):
                o = b0[u][:, 0:2 * DT * HS].rearrange("p (g t c) -> p g t c", g=2, c=HS)
                heads = slice(2 * (k % 2), 2 * (k % 2) + 2)
                iv, fl = inv[u][:, heads, :], flag[u][:, heads, :]
                dve.wait_ge(*attended.at(u, r, k))
                dve.reciprocal(iv, o[:, :, :, HD]).then_inc(numbers[u], 1)
                if k >= 2:
                    dve.wait_ge(*topped.at(u, r, k))
                    dve.tensor_scalar(fl, top[u][:, heads, :], 0.0, None, ALU.is_equal).then_inc(numbers[u], 1)
                    dve.wait_ge(*number(u, r, "top is 0", k))
                    dve.scalar_tensor_tensor(fl, low[u][:, heads, :], 0.0, fl, ALU.is_equal, ALU.mult)\
                       .then_inc(numbers[u], 1)
                    dve.wait_ge(*number(u, r, "row is 0", k))
                    dve.tensor_scalar(fl, fl, -1.0, 1.0, ALU.mult, ALU.add).then_inc(numbers[u], 1)
                    dve.wait_ge(*number(u, r, "row is not 0", k))
                    dve.tensor_tensor(iv, iv, fl, ALU.mult).then_inc(numbers[u], 1)
                dve.wait_ge(*number(u, r, "inverse" if k < 2 else "kept", k))
                dve.tensor_tensor(z[u][:, :].rearrange("p (t g c) -> p g t c", g=HG, c=HD)[:, heads, :, :],
                                  o[:, :, :, 0:HD], iv.unsqueeze(3).broadcast_to([128, 2, DT, HD]), ALU.mult)\
                   .then_inc(o_ready[u], 1)

            def u_gcn(r, u, layer):
                dve.wait_ge(*u_done.at(u, r, layer))
                dve.tensor_tensor(u_pair[u][:, :, :], b1[u][:, 0:2 * N].rearrange("p (a n) -> p a n", n=N),
                                  mask_pair[u][:, :, :], ALU.mult).then_inc(numbers[u], 1)
                dve.wait_ge(*number(u, r, "masked", layer))
                dve.tensor_tensor(e[u][:, :], u_pair[u][:, 0, :], u_pair[u][:, 1, :], ALU.add)\
                   .then_inc(u_ready[u], 1)

            def delta_gcn(r, u, layer):
                dve.wait_ge(*e_done.at(u, r, layer))
                dve.tensor_tensor(delta[u][:, :], e[u][:, :], adj_t[u][:, :], ALU.mult).then_inc(delta_done[u], 1)

            def u_di(r, u, layer):
                dve.wait_ge(*u_done.at(u, r, 2 + layer))
                dve.tensor_reduce(col(u, TOP), b1[u][:, 0:N], AX.X, ALU.max).then_inc(numbers[u], 1)
                dve.wait_ge(*number(u, r, "top of u", layer))
                dve.tensor_scalar(col(u, UBIAS), col(u, TOP), -1.0 / TEMPER, None, ALU.mult)\
                   .then_inc(u_bias_ready[u], 1)

            def delta_di(r, u, layer):
                dve.wait_ge(*e_done.at(u, r, 2 + layer))
                dve.tensor_tensor_reduce(out=delta[u][:, :], in0=e[u][:, :], in1=adj[u][:, :], scale=1.0,
                                         scalar=0.0, op0=ALU.mult, op1=ALU.add, accum_out=col(u, DSUM))\
                   .then_inc(delta_done[u], 1)
                dve.wait_ge(*delta_done.at(u, r, 2 + layer))
                dve.scalar_tensor_tensor(col(u, DENOM), col(u, ZSUM), 1e-10, col(u, DSUM), ALU.mult, ALU.add)\
                   .then_inc(numbers[u], 1)
                dve.wait_ge(*number(u, r, "sum 2", layer))
                dve.reciprocal(col(u, INV), col(u, DENOM)).then_inc(numbers[u], 1)
                dve.wait_ge(*number(u, r, "inverse sum 2", layer))
                dve.tensor_tensor(col(u, INV2), col(u, INV), col(u, INV), ALU.mult)\
                   .then_inc(numbers[u], 1)

            def turn_delta(r, u, layer):
                dve.wait_ge(*turned.at(u, r, TURNED.index(("turn_delta", layer))))
                dve.tensor_tensor(delta3[u], b1[u][:, 0:N].unsqueeze(1).broadcast_to([128, 3, N]), tri[:, :, :],
                                  ALU.mult).then_inc(delta3_done[u], 1)

            def moments(r, u, step, src):
                n = 2 * MOMENTS.index(step)
                dve.bn_stats(st6[u][:, :], src).then_inc(moments_done[u], 1)
                dve.wait_ge(*moments_done.at(u, r, n))
                dve.tensor_copy(col(u, TICK), powers[:, 0:1])
                dve.bn_aggr(mv[u][:, :], st6[u][:, :]).then_inc(moments_done[u], 1)
                dve.wait_ge(*moments_done.at(u, r, n + 1))

            def inner(r, u, k):
                bank = (b1 if k < 2 else b0)[u]
                dve.wait_ge(*mixed.at(u, r, k))
                if k < 2:
                    dve.tensor_scalar(col(u, DENOM), bank[:, D:D + 1], 1e-10, None, ALU.add)\
                       .then_inc(numbers[u], 1)
                    dve.wait_ge(*number(u, r, "sum", k))
                    dve.reciprocal(col(u, INV), col(u, DENOM)).then_inc(numbers[u], 1)
                    moments(r, u, ("inner", k), bank[:, 0:D])
                    dve.wait_ge(*number(u, r, "inverse sum", k))
                    dve.tensor_scalar(col(u, INV2), col(u, INV), col(u, INV), D / (D - 1.0), ALU.mult, ALU.mult)\
                       .then_inc(numbers[u], 1)
                    dve.wait_ge(*number(u, r, "inverse squared", k))
                    dve.tensor_tensor(col(u, VAR), mv[u][:, 1:2], col(u, INV2), ALU.mult)\
                       .then_inc(variance_done[u], 1)
                else:
                    moments(r, u, ("inner", k), bank[:, 0:D])
                    dve.wait_ge(*number(u, r, "inverse squared 2", k - 2))
                    dve.tensor_scalar(col(u, VAR), mv[u][:, 1:2], col(u, INV2), 1e-12, ALU.mult, ALU.add)\
                       .then_inc(variance_done[u], 1)
                dve.scalar_tensor_tensor(zc[u], bank[:, 0:D], mv[u][:, 0:1], rows[:, 2 * k, :], ALU.subtract, ALU.mult)\
                   .then_inc(numbers[u], 1)

            def gain(r, u, k):
                dve.wait_ge(*root_done.at(u, r, ROOTS.index(("inner", k))))
                if k < 2:
                    dve.tensor_scalar(col(u, BASE), col(u, ROOT), 1e-3, col(u, DENOM), ALU.add, ALU.mult)\
                       .then_inc(numbers[u], 1)
                    dve.wait_ge(*number(u, r, "gain base", k))
                    dve.reciprocal(col(u, GAIN), col(u, BASE)).then_inc(numbers[u], 1)
                else:
                    dve.tensor_tensor(col(u, GAIN), col(u, ROOT), col(u, INV), ALU.mult).then_inc(numbers[u], 1)
                dve.wait_ge(*number(u, r, "centred", k))
                dve.wait_ge(*number(u, r, "gain", k))
                dve.scalar_tensor_tensor(z[u][:, :], zc[u], col(u, GAIN), rows[:, 2 * k + 1, :], ALU.mult, ALU.add)\
                   .then_inc(inner_done[u], 1)

            def residual(r, u, layer):
                if layer == 0:
                    dve.wait_ge(*o_ready.at(u, r, 1))
                    dve.tensor_tensor(z[u][:, :], z[u][:, :], x[u][:, :], ALU.add).then_inc(residual_added[u], 1)
                elif layer < 3:
                    dve.wait_ge(*inner_done.at(u, r, 2 * layer - 1))
                    dve.scalar_tensor_tensor(z[u][:, :], z[u][:, :], 0.0, x[u][:, :], ALU.max, ALU.add)\
                       .then_inc(residual_added[u], 1)
                else:
                    dve.wait_ge(*projected.at(u, r, ORDER[L3_O]))
                    dve.scalar_tensor_tensor(z[u][:, :], b1[u][:, 0:D], 1.0 / WSCALE, x[u][:, :], ALU.mult,
                                             ALU.add).then_inc(residual_added[u], 1)
                dve.wait_ge(*residual_added.at(u, r, layer))
                moments(r, u, ("residual", layer), z[u][:, :])
                dve.tensor_scalar(col(u, VAR), mv[u][:, 1:2], 1e-5, None, ALU.add).then_inc(variance_done[u], 1)

            def norm(r, u, layer):
                dve.wait_ge(*root_done.at(u, r, ROOTS.index(("residual", layer))))
                dve.tensor_scalar(out[u] if layer == 3 else x[u][:, :], z[u][:, :], mv[u][:, 0:1], col(u, ROOT), ALU.subtract, ALU.mult)\
                   .then_inc(normed[u], 1)

            dve.wait_ge(consts_made, 6)
            dve.wait_ge(small_loaded, 48)
            dve.wait_ge(rows_loaded, 16)
            dve.wait_ge(dve_consts, DVE_CONSTS)

            def take(name, k, r, u):
                {"masks": masks, "turn": turn, "project": project, "scores": scores, "turn_p": turn_p,
                 "divide": divide, "u_gcn": u_gcn, "delta_gcn": delta_gcn, "u_di": u_di, "delta_di": delta_di,
                 "turn_delta": turn_delta, "inner": inner, "gain": gain, "residual": residual,
                 "norm": norm}[name](r, u, k)

            rounds(dve, VECTOR, take)


def kernel(**inputs):
    import numpy as _np
    import concourse.bacc as _bacc
    from concourse.bass_utils import run_bass_kernel_spmd as _run

    a = {k: _np.asarray(v) for k, v in inputs.items()}
    ws = [a["L0_gnn_Wq"], a["L0_gnn_Wk"], a["L0_gnn_Wv"]]
    for layer in range(2):
        ws += [a[f"L1_gnn_{n}"][layer].T for n in ("W_left", "W_right", "W_lin")]
    for layer in range(2):
        ws += [a[f"L2_gnn_{n}"][layer].T for n in ("Wl", "Ws", "Wr")]
    ws += [a[f"L3_gnn_{n}"].T for n in ("Wq", "Wk", "Wv", "Wo")]
    biases = [a["L0_gnn_bq"], a["L0_gnn_bk"], a["L0_gnn_bv"], a["L1_gnn_b_lin"][0], a["L1_gnn_b_lin"][1]]
    for layer in range(2):
        biases += [a[f"L2_gnn_{n}"][layer] for n in ("bl", "bs", "br")]
    biases += [a["L3_gnn_bv"], a["L3_gnn_bo"]]
    rows = []
    for layer in range(2):
        rows += [a["L1_gnn_ln_a"][layer], a["L1_gnn_ln_b"][layer]]
    for layer in range(2):
        rows += [a["L2_gnn_ln_w"][layer], a["L2_gnn_ln_b"][layer]]
    arrays = {
        "x_dram": _np.ascontiguousarray(a["x"]),
        "adj_dram": _np.ascontiguousarray(a["adj"]),
        "w_dram": _np.stack([_np.ascontiguousarray(w) for w in ws]),
        "bias_dram": _np.stack(biases),
        "rows_dram": _np.stack(rows),
        "beta_dram": a["L0_gnn_beta"].reshape(1),
    }
    nc = _bacc.Bacc("TRN2", target_bir_lowering=False, num_devices=1)
    args = [nc.dram_tensor(name, v.shape, F32, kind="ExternalInput").ap() for name, v in arrays.items()]
    out = nc.dram_tensor("out_dram", (B, N, D), F32, kind="ExternalOutput").ap()
    graph_layers(nc, *args, out)
    r = _run(nc, [arrays], core_ids=[0])
    return r.results[0]["out_dram"]
```

```python
import numpy as np
import concourse.bass as bass
from concourse import mybir
from contextlib import ExitStack

F32, F16 = mybir.dt.float32, mybir.dt.float16
ACT = mybir.ActivationFunctionType
ALU = mybir.AluOpType
AX = mybir.AxisListType

B, N, D = 64, 128, 384
H, HD = 12, 32
DT = D // 128
HG = 128 // HD
HS = HD + 1
UNITS = 4
ROUNDS = B // UNITS
assert B == UNITS * ROUNDS
WSCALE = 64.0
MASKED = -9000000000000000.0
TEMPER = float(np.sqrt(D))
BANK = 512

L0_Q, L0_K, L0_V = 0, 1, 2
L1_W = ((3, 4, 5), (6, 7, 8))
L2_W = ((9, 10, 11), (12, 13, 14))
L3_Q, L3_K, L3_V, L3_O = 15, 16, 17, 18
NW = 19
BIAS_OF = {L0_Q: 0, L0_K: 1, 5: 2, 8: 3, 9: 4, 10: 5, 11: 6, 12: 7, 13: 8, 14: 9, L3_V: 10}
NB = 11
NR = 10
X_BIAS = {0: 8, 5: 9}


PE, SCALAR, VECTOR, POOL, SYNC = "PE", "SCALAR", "VECTOR", "POOL", "SYNC"
PERIOD = UNITS * 54.00
TIMES = {
    ("turn", 0): {PE: 0.00, POOL: 2.54, SCALAR: 4.48, VECTOR: 6.77},
    ("masks", 0): {PE: 0.33, SCALAR: 1.35, POOL: 1.70, VECTOR: 7.24},
    ("project", 2): {PE: 10.78, SCALAR: 12.44, VECTOR: 13.18},
    ("project", 0): {PE: 12.68, SCALAR: 15.90, VECTOR: 17.07},
    ("project", 1): {PE: 15.33, SCALAR: 17.21, VECTOR: 17.78},
    ("scores", 0): {PE: 18.45, VECTOR: 19.77, SCALAR: 21.84},
    ("turn_p", 0): {PE: 24.06, SCALAR: 24.91, VECTOR: 25.80},
    ("attend", 0): {PE: 26.88},
    ("divide", 0): {VECTOR: 27.51},
    ("scores", 1): {PE: 28.21, VECTOR: 29.42, SCALAR: 31.48},
    ("turn_p", 1): {PE: 33.48, SCALAR: 34.33, VECTOR: 35.22},
    ("attend", 1): {PE: 36.29},
    ("divide", 1): {VECTOR: 36.93},
    ("residual", 0): {VECTOR: 37.43, POOL: 38.96},
    ("norm", 0): {VECTOR: 39.88},
    ("turn", 1): {PE: 40.47, SCALAR: 40.99, VECTOR: 41.56},
    ("project", 3): {PE: 42.23, SCALAR: 43.94, VECTOR: 45.25},
    ("project", 4): {PE: 43.74, SCALAR: 45.45, VECTOR: 46.02},
    ("u_gcn", 0): {PE: 46.69, VECTOR: 47.90, SCALAR: 48.76},
    ("project", 5): {PE: 47.70, SCALAR: 49.52},
    ("delta_gcn", 0): {VECTOR: 49.16},
    ("mix", 0): {PE: 50.09},
    ("inner", 0): {VECTOR: 50.94, POOL: 52.53},
    ("gain", 0): {VECTOR: 53.20},
    ("turn", 2): {PE: 54.45, SCALAR: 54.97, VECTOR: 55.54},
    ("project", 6): {PE: 56.40, SCALAR: 58.11, VECTOR: 59.34},
    ("project", 7): {PE: 58.01, SCALAR: 59.72, VECTOR: 60.29},
    ("u_gcn", 1): {PE: 61.49, VECTOR: 63.15, SCALAR: 64.04},
    ("project", 8): {PE: 63.15, SCALAR: 64.98},
    ("delta_gcn", 1): {VECTOR: 66.97},
    ("mix", 1): {PE: 68.36},
    ("inner", 1): {VECTOR: 69.21, POOL: 70.79},
    ("gain", 1): {VECTOR: 72.25},
    ("residual", 1): {VECTOR: 75.63, POOL: 77.17},
    ("norm", 1): {VECTOR: 78.30},
    ("turn", 3): {PE: 78.89, SCALAR: 79.60, VECTOR: 80.66},
    ("u_di", 0): {PE: 81.33, VECTOR: 82.03, SCALAR: 82.63},
    ("project", 9): {PE: 83.21, SCALAR: 85.04},
    ("project", 10): {PE: 85.85, SCALAR: 89.02},
    ("project", 11): {PE: 88.13, SCALAR: 89.95},
    ("delta_di", 0): {VECTOR: 88.91},
    ("turn_delta", 0): {PE: 89.75, VECTOR: 90.09},
    ("mix", 2): {PE: 90.75},
    ("inner", 2): {VECTOR: 96.03, POOL: 97.62},
    ("gain", 2): {VECTOR: 98.72},
    ("turn", 4): {PE: 100.25, SCALAR: 100.78, VECTOR: 101.35},
    ("u_di", 1): {PE: 103.32, VECTOR: 104.02, SCALAR: 104.61},
    ("project", 12): {PE: 104.74, SCALAR: 106.57},
    ("delta_di", 1): {VECTOR: 106.33},
    ("project", 13): {PE: 106.37, SCALAR: 108.19},
    ("project", 14): {PE: 108.77, SCALAR: 112.85},
    ("turn_delta", 1): {PE: 111.90, VECTOR: 112.87},
    ("mix", 3): {PE: 113.54},
    ("inner", 3): {VECTOR: 115.75, POOL: 117.35},
    ("gain", 3): {VECTOR: 119.11},
    ("residual", 2): {VECTOR: 119.63, POOL: 121.17},
    ("norm", 2): {VECTOR: 122.62},
    ("turn", 5): {PE: 125.00, SCALAR: 125.58, VECTOR: 127.30, POOL: 131.88},
    ("project", 17): {PE: 128.91, SCALAR: 131.59, VECTOR: 132.69},
    ("project", 15): {PE: 130.54, SCALAR: 132.25, VECTOR: 136.89},
    ("project", 16): {PE: 133.36, SCALAR: 135.07, VECTOR: 136.43},
    ("scores", 2): {PE: 138.84, VECTOR: 140.04, SCALAR: 144.32},
    ("turn_p", 2): {PE: 146.70, SCALAR: 147.55, VECTOR: 148.44},
    ("attend", 2): {PE: 149.51},
    ("divide", 2): {VECTOR: 151.42},
    ("scores", 3): {PE: 153.24, VECTOR: 164.01, SCALAR: 168.09},
    ("turn_p", 3): {PE: 170.49, SCALAR: 171.34, VECTOR: 172.23},
    ("attend", 3): {PE: 174.23},
    ("divide", 3): {VECTOR: 175.64},
    ("turn", 6): {PE: 177.00, SCALAR: 177.52, VECTOR: 178.59},
    ("project", 18): {PE: 181.45},
    ("residual", 3): {VECTOR: 184.96, POOL: 214.99},
    ("norm", 3): {VECTOR: 216.24},
}
TIMES[("store", 0)] = {SYNC: TIMES[("norm", 3)][VECTOR] + 0.3}
TIMES[("load", 0)] = {SYNC: 0.0}


def steps_of(engine, *names):
    return sorted((s for s in TIMES if engine in TIMES[s] and (not names or s[0] in names)),
                  key=lambda s: TIMES[s][engine])


def body(engine):
    at = []
    for u in range(UNITS):
        for step in steps_of(engine):
            t = TIMES[step][engine] + PERIOD * u / UNITS
            at.append((t % PERIOD, *step, u, int(t >= PERIOD)))
    return [x[1:] for x in sorted(at)]


STAGES, FIRST_WEIGHTS = 3, 3
WEIGHT_TIMES = {w: 2.0 + 5.2 * (w - FIRST_WEIGHTS) for w in range(FIRST_WEIGHTS, NW)}
LAST_WEIGHT = max(WEIGHT_TIMES.values())
assert LAST_WEIGHT + 3.0 < 2 * PERIOD / UNITS


def first_round(engine):
    at = [(TIMES[step][engine] + PERIOD * u / UNITS, *step, u) for u in range(UNITS) for step in steps_of(engine)
          if TIMES[step][engine] + PERIOD * u / UNITS < PERIOD]
    if engine in (SCALAR, VECTOR):
        at += [(t + (engine == VECTOR), "weight", w, 0) for w, t in WEIGHT_TIMES.items()]
    if engine in (SCALAR, VECTOR, PE):
        at.append((LAST_WEIGHT + 2.5, "stages_free", 0, 0))
    assert all(t + 1.0 < TIMES["project", w][PE] for w, t in WEIGHT_TIMES.items())
    return [x[1:] for x in sorted(at)]


class Signal:

    def __init__(self, ctx, nc, name, per_round=1, step=1, primed=0):
        self.sems = [ctx.enter_context(nc.semaphore(f"{name}_{u}")) for u in range(UNITS)]
        self.per_round, self.step, self.primed = per_round, step, primed

    def prime(self, eng):
        assert self.primed == 1
        for sem in self.sems:
            eng.sem_inc(sem, 1)

    def __getitem__(self, u):
        return self.sems[u]

    def at(self, u, i, k=0):
        return self.sems[u], i * (self.per_round * self.step) + ((k + 1) * self.step + self.primed)

    def before(self, u, i):
        assert self.primed == 1
        return self.sems[u], i * (self.per_round * self.step) + 1


def graph_layers(nc, x_d, adj_d, w_d, bias_d, rows_d, beta_d, out_d):
    ctx = ExitStack()
    with ctx:
        def sb(name, shape, dt=F32):
            return ctx.enter_context(nc.sbuf_tensor(name, shape, dt))

        def per_unit(name, shape, dt=F32):
            return [sb(f"{name}_{u}", shape, dt) for u in range(UNITS)]

        def sem(name):
            return ctx.enter_context(nc.semaphore(name))

        def signal(name, per_round=1, step=1, primed=0):
            return Signal(ctx, nc, name, per_round, step, primed)

        w_hi = sb("w_hi", [128, NW, DT, D], F16)
        w_lo = sb("w_lo", [128, NW, DT, D], F16)
        bias_rows = sb("bias_rows", [128, NB, D], F16)
        ones = sb("ones", [128, 128], F16)
        rows = sb("rows", [128, NR, D])
        ident = sb("ident", [128, 128])
        tri = sb("tri", [128, 3, 128])
        tri_temper = sb("tri_temper", [128, 2, 128])
        beta = sb("beta", [128, 1])
        CONSTANTS = (0.5, -0.5, 1e-5, 1e-10, 1e-12)
        HALF, MINUS_HALF, LN_EPS, DEN_EPS, INNER_EPS = range(len(CONSTANTS))
        numbers_in = sb("numbers_in", [128, len(CONSTANTS)])

        adj = per_unit("adj", [128, N])
        adj_t = per_unit("adj_t", [128, N])
        mask_bias = per_unit("mask_bias", [128, N])
        mask_pair = per_unit("mask_pair", [128, 2, N])
        x = per_unit("x", [128, D])
        z = per_unit("z", [128, D])
        t_hi = per_unit("t_hi", [128, DT, N], F16)
        t_lo = per_unit("t_lo", [128, DT, N], F16)
        v_hi = per_unit("v_hi", [128, H, HS], F16)
        v_lo = per_unit("v_lo", [128, H, HS], F16)
        top = per_unit("top", [128, HG, DT])
        low = per_unit("low", [128, HG, DT])
        inv = per_unit("inv", [128, HG, DT])
        flag = per_unit("flag", [128, HG, DT])
        u_pair = per_unit("u_pair", [128, 2, N])
        e = per_unit("e", [128, N])
        delta = per_unit("delta", [128, N])
        st6 = per_unit("st6", [128, 6])
        mv = per_unit("mv", [128, 2])
        small = per_unit("small", [128, 12])
        VAR, ROOT, DENOM, DENOM3, EPS, BASE, GAIN, TOP, UBIAS, ZSUM, DSUM, TICK = range(12)

        def col(u, c):
            return small[u][:, c:c + 1]

        AB = DT * N // 2
        ab = sb("ab", [128, UNITS * 4 * AB])
        a_hi, a_lo, b_hi, b_lo = (
            [ab[:, (4 * u + n) * AB:(4 * u + n + 1) * AB].bitcast(F16).rearrange("p (t n) -> p t n", n=N)
             for u in range(UNITS)] for n in range(4))
        SCORES, PROJ = 2 * DT * N, 3 * (D + 1)
        shared = sb("shared", [128, UNITS * (SCORES + PROJ)])
        scores_at = [shared[:, u * SCORES:(u + 1) * SCORES] for u in range(UNITS)]
        proj_at = [shared[:, UNITS * SCORES + u * PROJ:UNITS * SCORES + (u + 1) * PROJ] for u in range(UNITS)]
        score = [a.rearrange("p (g t n) -> p g t n", g=2, t=DT) for a in scores_at]
        delta3 = [a[:, 0:3 * N].rearrange("p (m n) -> p m n", m=3) for a in scores_at]
        zc = [a[:, 3 * N:3 * N + D] for a in scores_at]
        out = zc
        proj = [a.rearrange("p (m d) -> p m d", m=3) for a in proj_at]
        p_hi, p_lo = ([a[:, D + 1 + n * DT * N:D + 1 + (n + 1) * DT * N].bitcast(F16)
                        .rearrange("p (g t n) -> p g t n", g=2, t=DT) for a in proj_at] for n in range(2))
        bias_stage = shared[:, 0:NB * D].rearrange("p (b d) -> p b d", d=D)
        assert NB * D <= UNITS * SCORES + 2 * PROJ and DT * D <= min(PROJ, 2 * 4 * AB)
        w_stage = [ab[:, 2 * 4 * AB:2 * 4 * AB + DT * D], proj_at[2][:, 0:DT * D], proj_at[3][:, 0:DT * D]]

        banks = [ctx.enter_context(nc.psum_tensor(f"banks_{u}", [128, 2, BANK], F32)) for u in range(UNITS)]
        b0 = [a[:, 0, :] for a in banks]
        b1 = [a[:, 1, :] for a in banks]
        blocks = [a[:, :, 0:D].rearrange("p g (t n) -> p g t n", n=N) for a in banks]

        w_loaded = [sem(f"w_loaded_{slot}") for slot in range(STAGES)]
        late_ones = sem("late_ones")
        w_hi_made, w_lo_made = sem("w_hi_made"), sem("w_lo_made")
        small_loaded = sem("small_loaded")
        consts_cleared, consts_made = sem("consts_cleared"), sem("consts_made")
        dve_consts = sem("dve_consts")
        bias_hi_made, bias_made = sem("bias_hi_made"), sem("bias_made")
        rows_loaded, bias_rows_cleared = sem("rows_loaded"), sem("bias_rows_cleared")
        loaded = signal("loaded", step=32)
        stored = signal("stored", step=16, primed=1)
        TURNED = steps_of(PE, "masks", "turn", "turn_delta")
        turned = signal("turned", len(TURNED))
        projected = signal("projected", NW)
        scored = signal("scored", 4)
        p_turned = signal("p_turned", 4)
        attended = signal("attended", 4)
        u_done = signal("u_done", 4)
        mixed = signal("mixed", 4)
        adjt_done = signal("adjt_done")
        t_hi_done = signal("t_hi_done", 7)
        proj_hi_done = signal("proj_hi_done", 18)
        exp_done = signal("exp_done", 4)
        p_hi_done = signal("p_hi_done", 4)
        e_done = signal("e_done", 4)
        masks_done = signal("masks_done", 2)
        t_lo_done = signal("t_lo_done", 7)
        proj_lo_done = signal("proj_lo_done", 10)
        biased = signal("biased", 4)
        topped = signal("topped", 4)
        p_lo_done = signal("p_lo_done", 4)
        o_ready = signal("o_ready", 4)
        residual_added = signal("residual_added", 4, primed=1)
        u_ready = signal("u_ready", 2)
        u_bias_ready = signal("u_bias_ready", 2)
        delta_done = signal("delta_done", 4)
        delta3_done = signal("delta3_done", 2)
        MOMENTS = steps_of(VECTOR, "inner", "residual")
        moments_done = signal("moments_done", 2 * 8)
        inner_done = signal("inner_done", 4)
        normed = signal("normed", 4)
        NUMBERS = []
        for name_, k_ in steps_of(VECTOR):
            NUMBERS += [(what, k_) for what in {
                "scores": ("minimum",) if k_ >= 2 else (),
                "divide": ("inverse",) if k_ < 2 else ("low is not 0", "row is not 0", "inverse", "kept"),
                "u_gcn": ("masked",), "u_di": ("top of u",),
                "inner": ("sum", "centred") if k_ < 2 else ("centred",),
                "gain": ("gain base", "gain") if k_ < 2 else ()}.get(name_, ())]
        numbers = signal("numbers", len(NUMBERS))
        root_done = signal("root_done", 8)
        ROOTS = steps_of(POOL, "inner", "residual")
        pair_done = signal("pair_done", 2)
        x_biased = signal("x_biased", 2)
        SUMS = []
        for name_, k_ in ROOTS:
            SUMS += [(what, name_, k_) for what in (("part of sum", "sum", "sum squared", "constant", "variance")
                     if name_ == "inner" and k_ >= 2 else ("variance",) if name_ == "residual" else ())]
        sums = signal("sums", len(SUMS))

        ORDER = {w: n for n, (_, w) in enumerate(steps_of(PE, "project"))}
        HI = {w: n for n, (_, w) in enumerate(steps_of(SCALAR, "project"))}
        LO = {w: n for n, (_, w) in enumerate(steps_of(VECTOR, "project"))}

        def number(u, r, what, k):
            return numbers.at(u, r, NUMBERS.index((what, k)))

        def constant(c):
            return numbers_in[:, c:c + 1]

        def rounds(eng, engine, take):
            order = body(engine)
            for name, k, u in first_round(engine):
                take(name, k, 0, u)
            with eng.Fori(1, ROUNDS) as i:
                for n, (name, k, u, back) in enumerate(order):
                    if n % 8 == 0:
                        now = nc.snap(i, engines=[eng.engine])
                    take(name, k, now - back, u)
            for name, k, u, back in order:
                if back:
                    take(name, k, ROUNDS - 1, u)

        block = ctx.enter_context(nc.Block())

        DVE_CONSTS = 1 + len(CONSTANTS) + 2 * UNITS + 2

        ACROSS = (L0_Q, L0_K, *L1_W[0][:2], *L1_W[1][:2], L3_Q, L3_K)
        TURN_OF = {L0_Q: 0, L0_K: 0, L0_V: 0, **{w: 1 + n for n in range(2) for w in L1_W[n]},
                   **{w: 3 + n for n in range(2) for w in L2_W[n]}, L3_Q: 5, L3_K: 5, L3_V: 5, L3_O: 6}

        def across(bank):
            return bank[:, 0:D].rearrange("p (t n) -> p t n", n=N)

        def bank_of(u, w):
            in_b1 = (L0_Q, L1_W[0][0], L1_W[1][0], L2_W[0][1], L2_W[1][1], L3_Q, L3_O)
            return (b1 if w in in_b1 else b0)[u]

        def place_of(u, w):
            bank = bank_of(u, w)
            if w in ACROSS:
                scale = {L0_Q: HD ** -0.5, L3_Q: D ** -0.5}.get(w, 1.0)
                return (a_hi if bank is b1[u] else b_hi)[u], across(bank), scale
            if w in (L0_V, L3_V):
                return v_hi[u][:, :, 0:HD], bank[:, 0:D].rearrange("p (h n) -> p h n", n=HD), 1.0
            m = 0 if w in (L1_W[0][2], L1_W[1][2]) else (w - L2_W[0][0]) % 3
            return proj[u][:, m, 0:D], bank[:, 0:D], 1.0

        def low_of(u, w):
            if w in ACROSS:
                return (a_lo if bank_of(u, w) is b1[u] else b_lo)[u]
            return v_lo[u][:, :, 0:HD]

        @block.sync
        def _(sp):
            stored.prime(sp)

            def load_weight(w, slot):
                sp.dma_start(w_stage[slot].rearrange("p (t o) -> p t o", o=D), w_d[w].rearrange("(t p) o -> p t o", p=128))\
                  .then_inc(w_loaded[slot], 16)

            def load(r, u):
                sp.dma_start(x[u][:, :], x_d[r * UNITS + u]).then_inc(loaded[u], 16)
                sp.dma_start(adj[u][:, :], adj_d[r * UNITS + u]).then_inc(loaded[u], 16)

            load(0, 0)
            for w in range(STAGES):
                load_weight(w, w)
            sp.dma_start(beta[:, :], beta_d.partition_broadcast(128)).then_inc(small_loaded, 16)
            for row in (0, 32):
                sp.dma_start(bias_stage[row:row + 1, :, :], bias_d.rearrange("(a b) d -> a b d", a=1))\
                  .then_inc(small_loaded, 16)
            load(0, 1)

            def load_weights(g):
                for slot in range(STAGES):
                    sp.wait_ge(w_lo_made, g * STAGES + (slot - STAGES + 1))
                    load_weight(g * STAGES + slot, slot)

            load_weights(1)
            sp.dma_start(rows[:, :, :], rows_d.rearrange("r d -> (r d)").partition_broadcast(128)
                         .rearrange("p (r d) -> p r d", d=D)).then_inc(rows_loaded, 16)
            with sp.Fori(2, NW // STAGES) as g:
                load_weights(g)
            assert NW % STAGES == 1
            sp.wait_ge(w_lo_made, NW - STAGES)
            load_weight(NW - 1, 0)
            for u in range(2, UNITS):
                load(0, u)

            def take(name, k, r, u):
                if name == "load" and not isinstance(r, int):
                    sp.wait_ge(*residual_added.before(u, r))
                    load(r, u)
                if name == "store":
                    sp.wait_ge(*normed.at(u, r, 3))
                    sp.dma_start(out_d[r * UNITS + u], out[u]).then_inc(stored[u], 16)

            rounds(sp, SYNC, take)
            for u in range(UNITS):
                sp.wait_ge(*stored.before(u, ROUNDS))

        @block.gpsimd
        def _(pool):
            pool.memset(bias_rows[:, :, :], 0.0).then_inc(bias_rows_cleared, 1)
            pool.memset(ident[:, :], 0.0).then_inc(consts_cleared, 1)
            pool.memset(tri[:, :, :], 1.0).then_inc(consts_cleared, 1)
            pool.memset(tri_temper[:, :, :], 1.0 / TEMPER).then_inc(consts_cleared, 1)
            pool.wait_ge(consts_cleared, 3)
            pool.affine_select(out=ident[:, :], in_=ident[:, :], compare_op=ALU.not_equal, fill=1.0, base=0,
                               pattern=[[-1, 128]], channel_multiplier=1).then_inc(consts_made, 1)
            for m, op, sign in ((0, ALU.is_gt, 1), (1, ALU.is_equal, 1), (2, ALU.is_gt, -1)):
                pool.affine_select(out=tri[:, m, :], in_=tri[:, m, :], compare_op=op, fill=0.0, base=0,
                                   pattern=[[-sign, 128]], channel_multiplier=sign).then_inc(consts_made, 1)
            for m, op, sign in ((0, ALU.is_ge, 1), (1, ALU.is_gt, -1)):
                pool.affine_select(out=tri_temper[:, m, :], in_=tri_temper[:, m, :], compare_op=op, fill=0.0, base=0,
                                   pattern=[[-sign, 128]], channel_multiplier=sign).then_inc(consts_made, 1)
            pool.wait_ge(rows_loaded, 16)
            pool.wait_ge(dve_consts, len(CONSTANTS))
            pool.wait_ge(consts_made, 6)

            def masks(r, u):
                pool.wait_ge(*adjt_done.at(u, r))
                pool.tensor_tensor(mask_pair[u][:, 0, :], adj_t[u][:, :], tri_temper[:, 0, :], ALU.mult)\
                    .then_inc(pair_done[u], 1)
                pool.tensor_tensor(mask_pair[u][:, 1, :], adj[u][:, :], tri_temper[:, 1, :], ALU.mult)\
                    .then_inc(pair_done[u], 1)

            def root(r, u, name, k):
                def step(what, out, a, b, op):
                    pool.tensor_tensor(col(u, out), a, b, op).then_inc(sums[u], 1)
                    pool.wait_ge(*sums.at(u, r, SUMS.index((what, name, k))))

                if name == "inner" and k >= 2:
                    pool.wait_ge(*delta_done.at(u, r, k))
                    step("part of sum", DENOM, col(u, ZSUM), constant(DEN_EPS), ALU.mult)
                    step("sum", DENOM, col(u, DENOM), col(u, DSUM), ALU.add)
                    step("sum squared", DENOM, col(u, DENOM), col(u, DENOM), ALU.mult)
                    step("constant", EPS, col(u, DENOM), constant(INNER_EPS), ALU.mult)
                pool.wait_ge(*moments_done.at(u, r, 2 * MOMENTS.index((name, k)) + 1))
                if name == "inner" and k < 2:
                    pool.tensor_tensor(col(u, ROOT), mv[u][:, 1:2], constant(HALF), ALU.pow).then_inc(root_done[u], 1)
                else:
                    step("variance", VAR, mv[u][:, 1:2], col(u, EPS) if name == "inner" else constant(LN_EPS), ALU.add)
                    pool.tensor_tensor(col(u, ROOT), col(u, VAR), constant(MINUS_HALF), ALU.pow)\
                        .then_inc(root_done[u], 1)

            def turn(r, u, k):
                pool.wait_ge(*turned.at(u, r, TURNED.index(("turn", k))))
                pool.tensor_tensor(x[u][:, :], x[u][:, :], rows[:, X_BIAS[k], :], ALU.add).then_inc(x_biased[u], 1)

            def take(name, k, r, u):
                if name == "masks":
                    masks(r, u)
                elif name == "turn":
                    turn(r, u, k)
                else:
                    root(r, u, name, k)

            rounds(pool, POOL, take)

        @block.scalar
        def _(act):
            act.wait_ge(small_loaded, 48)
            act.wait_ge(bias_rows_cleared, 1)
            for row in (0, 32):
                act.activation(bias_rows[row:row + 1, :, :], bias_stage[row:row + 1, :, :], ACT.Copy, scale=WSCALE)\
                   .then_inc(bias_hi_made, 1)

            def weight(r, u, w):
                act.wait_ge(w_loaded[w % STAGES], 16 * (w // STAGES) + 16)
                act.activation(w_hi[:, w, :, :].rearrange("p t o -> p (t o)"), w_stage[w % STAGES], ACT.Copy, scale=WSCALE)\
                   .then_inc(w_hi_made, 1)

            for w in range(FIRST_WEIGHTS):
                weight(0, 0, w)
            act.wait_ge(bias_made, 1)

            def stages_free(r, u, k):
                act.wait_ge(w_lo_made, NW)

            def masks(r, u, k):
                act.wait_ge(*turned.at(u, r, TURNED.index(("masks", 0))))
                act.activation(adj_t[u][:, :], b1[u][:, 0:N], ACT.Copy).then_inc(adjt_done[u], 1)

            def turn(r, u, k):
                act.wait_ge(*turned.at(u, r, TURNED.index(("turn", k))))
                act.activation(t_hi[u][:, :, :], across(b0[u]), ACT.Relu if k in (2, 4) else ACT.Copy)\
                   .then_inc(t_hi_done[u], 1)

            def project(r, u, w):
                act.wait_ge(*projected.at(u, r, ORDER[w]))
                dst, src, scale = place_of(u, w)
                act.activation(dst, src, ACT.Copy, scale=scale / WSCALE).then_inc(proj_hi_done[u], 1)

            def scores(r, u, k):
                act.wait_ge(*topped.at(u, r, k))
                for g2 in range(2):
                    for t in range(DT):
                        last = act.activation(score[u][:, g2, t, :], score[u][:, g2, t, :], ACT.Exp,
                                              bias=top[u][:, 2 * (k % 2) + g2, t:t + 1])
                last.then_inc(exp_done[u], 1)

            def turn_p(r, u, k):
                act.wait_ge(*p_turned.at(u, r, k))
                act.activation(p_hi[u], blocks[u], ACT.Copy).then_inc(p_hi_done[u], 1)

            def u_gcn(r, u, layer):
                act.wait_ge(*u_ready.at(u, r, layer))
                act.activation(e[u][:, :], e[u][:, :], ACT.Exp).then_inc(e_done[u], 1)

            def u_di(r, u, layer):
                act.wait_ge(*u_bias_ready.at(u, r, layer))
                act.activation(e[u][:, :], b1[u][:, 0:N], ACT.Exp, bias=col(u, UBIAS), scale=1.0 / TEMPER,
                               accum_out=col(u, ZSUM)).then_inc(e_done[u], 1)

            def take(name, k, r, u):
                {"weight": weight, "stages_free": stages_free, "masks": masks, "turn": turn, "project": project,
                 "scores": scores, "turn_p": turn_p, "u_gcn": u_gcn, "u_di": u_di}[name](r, u, k)

            rounds(act, SCALAR, take)

        @block.tensor
        def _(pe):
            def transpose_tiles(u, src):
                for t in range(DT):
                    last = pe.transpose(b0[u][:, t * N:(t + 1) * N], src[:, t * 128:(t + 1) * 128], ident[:, :])
                return last

            def masks(r, u, k):
                pe.wait_ge(*loaded.at(u, r))
                pe.wait_ge(*residual_added.before(u, r))
                pe.transpose(b1[u][:, 0:N], adj[u][:, :], ident[:, :]).then_inc(turned[u], 1)

            def turn(r, u, k):
                if k == 0:
                    pe.wait_ge(*loaded.at(u, r))
                    pe.wait_ge(*residual_added.before(u, r))
                    src = x
                elif k in (2, 4):
                    pe.wait_ge(*inner_done.at(u, r, k - 2))
                    src = z
                elif k in (1, 3, 5):
                    pe.wait_ge(*normed.at(u, r, k // 2))
                    src = x
                else:
                    pe.wait_ge(*o_ready.at(u, r, 3))
                    src = z
                transpose_tiles(u, src[u]).then_inc(turned[u], 1)

            def project_across(u, w, out):
                for t in range(DT):
                    o = out[:, t * N:(t + 1) * N]
                    cols = slice(t * 128, (t + 1) * 128)
                    for k in range(DT):
                        pe.matmul(o, lhsT=w_hi[:, w, k, cols], rhs=t_hi[u][:, k, :], start=(k == 0), stop=False)
                        pe.matmul(o, lhsT=w_hi[:, w, k, cols], rhs=t_lo[u][:, k, :], start=False, stop=False)
                        last = pe.matmul(o, lhsT=w_lo[:, w, k, cols], rhs=t_hi[u][:, k, :], start=False,
                                         stop=(k == DT - 1 and w not in BIAS_OF))
                    if w in BIAS_OF:
                        last = pe.matmul(o, lhsT=bias_rows[:, BIAS_OF[w], cols], rhs=ones[:, :], start=False, stop=True)
                last.then_inc(projected[u], 1)

            def project_natural(u, w, out):
                for k in range(DT):
                    pe.matmul(out, lhsT=t_hi[u][:, k, :], rhs=w_hi[:, w, k, :], start=(k == 0), stop=False)
                    pe.matmul(out, lhsT=t_hi[u][:, k, :], rhs=w_lo[:, w, k, :], start=False, stop=False)
                    last = pe.matmul(out, lhsT=t_lo[u][:, k, :], rhs=w_hi[:, w, k, :], start=False,
                                     stop=(k == DT - 1 and w not in BIAS_OF))
                if w in BIAS_OF:
                    last = pe.matmul(out, lhsT=ones[:, :], rhs=bias_rows[:, BIAS_OF[w], :], start=False, stop=True)
                last.then_inc(projected[u], 1)

            def project(r, u, w):
                if isinstance(r, int) and r == 0 and u == 0:
                    pe.wait_ge(w_lo_made, w + 1)
                pe.wait_ge(*t_lo_done.at(u, r, TURN_OF[w]))
                if w == L0_Q:
                    pe.wait_ge(*adjt_done.at(u, r))
                if w in (L0_K, L3_K):
                    pe.wait_ge(*proj_lo_done.at(u, r, LO[w + 1]))
                if w in (L1_W[0][2], L1_W[1][2]):
                    pe.wait_ge(*proj_lo_done.at(u, r, LO[w - 1]))
                if w in (L2_W[0][1], L2_W[1][1]):
                    pe.wait_ge(*e_done.at(u, r, 2 + (w == L2_W[1][1])))
                if w in (L2_W[0][2], L2_W[1][2]):
                    pe.wait_ge(*proj_hi_done.at(u, r, HI[w - 2]))
                if w in ACROSS:
                    project_across(u, w, bank_of(u, w))
                else:
                    project_natural(u, w, bank_of(u, w)[:, 0:D])

            def product(out, ahi, alo, bhi, blo):
                for k in range(DT):
                    pe.matmul(out, lhsT=ahi[:, k, :], rhs=bhi[:, k, :], start=(k == 0), stop=False)
                    pe.matmul(out, lhsT=ahi[:, k, :], rhs=blo[:, k, :], start=False, stop=False)
                    last = pe.matmul(out, lhsT=alo[:, k, :], rhs=bhi[:, k, :], start=False, stop=(k == DT - 1))
                return last

            def scores(r, u, k):
                pe.wait_ge(*proj_lo_done.at(u, r, max(LO[w] for w in ((L0_Q, L0_K, L0_V) if k < 2 else
                                                                      (L3_Q, L3_K, L3_V)))))
                if k % 2:
                    pe.wait_ge(*o_ready.at(u, r, k - 1))
                for t in range(DT):
                    for qp, kp, n in ((a_hi, b_hi, 0), (a_hi, b_lo, 1), (a_lo, b_hi, 2)):
                        for g2 in range(2):
                            rows_ = slice(HD * (2 * (k % 2) + g2), HD * (2 * (k % 2) + g2) + HD)
                            last = pe.matmul(banks[u][:, g2, t * N:(t + 1) * N], lhsT=qp[u][rows_, t, :],
                                             rhs=kp[u][rows_, t, :], start=(n == 0), stop=(n == 2))
                last.then_inc(scored[u], 1)

            def turn_p(r, u, k):
                pe.wait_ge(*exp_done.at(u, r, k))
                for g2 in range(2):
                    for t in range(DT):
                        last = pe.transpose(banks[u][:, g2, t * N:(t + 1) * N], score[u][:, g2, t, :], ident[:, :])
                last.then_inc(p_turned[u], 1)

            def attend(r, u, k):
                pe.wait_ge(*p_lo_done.at(u, r, k))
                for g2 in range(2):
                    for t in range(DT):
                        h = HG * t + 2 * (k % 2) + g2
                        o = b0[u][:, (DT * g2 + t) * HS:(DT * g2 + t + 1) * HS]
                        pe.matmul(o, lhsT=p_hi[u][:, g2, t, :], rhs=v_hi[u][:, h, :], start=True, stop=False)
                        pe.matmul(o, lhsT=p_hi[u][:, g2, t, :], rhs=v_lo[u][:, h, :], start=False, stop=False)
                        last = pe.matmul(o, lhsT=p_lo[u][:, g2, t, :], rhs=v_hi[u][:, h, :], start=False, stop=True)
                last.then_inc(attended[u], 1)

            def u_gcn(r, u, layer):
                pe.wait_ge(*proj_lo_done.at(u, r, max(LO[w] for w in L1_W[layer][:2])))
                product(b1[u][:, 0:N], a_hi[u], a_lo[u], t_hi[u], t_lo[u])
                product(b1[u][:, N:2 * N], b_hi[u], b_lo[u], t_hi[u], t_lo[u]).then_inc(u_done[u], 1)

            def u_di(r, u, layer):
                pe.wait_ge(*t_lo_done.at(u, r, 3 + layer))
                product(b1[u][:, 0:N], t_hi[u], t_lo[u], t_hi[u], t_lo[u]).then_inc(u_done[u], 1)

            def turn_delta(r, u, layer):
                pe.wait_ge(*delta_done.at(u, r, 2 + layer))
                pe.wait_ge(*proj_hi_done.at(u, r, HI[L2_W[layer][1]]))
                pe.transpose(b1[u][:, 0:N], delta[u][:, :], ident[:, :]).then_inc(turned[u], 1)

            def mix(r, u, k):
                if k < 2:
                    pe.wait_ge(*proj_hi_done.at(u, r, HI[L1_W[k][2]]))
                    pe.wait_ge(*delta_done.at(u, r, k))
                    pe.matmul(b1[u][:, 0:D + 1], lhsT=delta[u][:, :], rhs=proj[u][:, 0, :], start=True, stop=True)\
                      .then_inc(mixed[u], 1)
                else:
                    pe.wait_ge(*proj_hi_done.at(u, r, max(HI[w] for w in L2_W[k - 2])))
                    pe.wait_ge(*delta3_done.at(u, r, k - 2))
                    for m in range(3):
                        last = pe.matmul(b0[u][:, 0:D], lhsT=delta3[u][:, m, :], rhs=proj[u][:, m, 0:D],
                                         start=(m == 0), stop=(m == 2))
                    last.then_inc(mixed[u], 1)

            def stages_free(r, u, k):
                pe.wait_ge(w_lo_made, NW)
                pe.wait_ge(late_ones, 2)

            pe.wait_ge(bias_made, 1)
            pe.wait_ge(consts_made, 6)
            pe.wait_ge(dve_consts, DVE_CONSTS)

            def take(name, k, r, u):
                {"stages_free": stages_free, "masks": masks, "turn": turn, "project": project, "scores": scores,
                 "turn_p": turn_p, "attend": attend, "u_gcn": u_gcn, "u_di": u_di, "turn_delta": turn_delta, "mix": mix}[name](r, u, k)

            rounds(pe, PE, take)

        @block.vector
        def _(dve):
            residual_added.prime(dve)
            for c, value in enumerate(CONSTANTS):
                dve.memset(constant(c), value).then_inc(dve_consts, 1)
            dve.memset(ones[:, :], 1.0).then_inc(dve_consts, 1)
            for u in range(UNITS):
                dve.memset(v_hi[u][:, :, HD:HS], 1.0).then_inc(dve_consts, 1)
                dve.memset(v_lo[u][:, :, HD:HS], 0.0).then_inc(dve_consts, 1)
            dve.wait_ge(bias_hi_made, 2)
            dve.scalar_tensor_tensor(bias_rows[32:33, :, :], bias_stage[32:33, :, :], WSCALE, bias_rows[32:33, :, :],
                                     ALU.mult, ALU.subtract).then_inc(bias_made, 1)
            dve.wait_ge(bias_made, 1)
            for u in range(2):
                dve.memset(proj[u][:, 0, D:D + 1], 1.0).then_inc(dve_consts, 1)

            def weight(r, u, w):
                dve.wait_ge(w_hi_made, w + 1)
                dve.scalar_tensor_tensor(w_lo[:, w, :, :].rearrange("p t o -> p (t o)"), w_stage[w % STAGES], WSCALE,
                                         w_hi[:, w, :, :].rearrange("p t o -> p (t o)"), ALU.mult, ALU.subtract)\
                   .then_inc(w_lo_made, 1)

            for w in range(FIRST_WEIGHTS):
                weight(0, 0, w)

            def stages_free(r, u, k):
                dve.wait_ge(w_lo_made, NW)
                for late in range(2, UNITS):
                    dve.memset(proj[late][:, 0, D:D + 1], 1.0).then_inc(late_ones, 1)

            def masks(r, u, k):
                dve.wait_ge(*loaded.at(u, r))
                dve.tensor_scalar(mask_bias[u][:, :], adj[u][:, :], 0.0, MASKED, ALU.is_le, ALU.mult)\
                   .then_inc(masks_done[u], 1)
                dve.wait_ge(*masks_done.at(u, r, 0))
                dve.scalar_tensor_tensor(mask_bias[u][:, :], adj[u][:, :], beta[:, 0:1], mask_bias[u][:, :],
                                         ALU.mult, ALU.add).then_inc(masks_done[u], 1)

            def turn(r, u, k):
                dve.wait_ge(*t_hi_done.at(u, r, k))
                if k in (2, 4):
                    dve.scalar_tensor_tensor(t_lo[u][:, :, :], across(b0[u]), 0.0, t_hi[u][:, :, :], ALU.max,
                                             ALU.subtract).then_inc(t_lo_done[u], 1)
                else:
                    dve.tensor_tensor(t_lo[u][:, :, :], across(b0[u]), t_hi[u][:, :, :], ALU.subtract)\
                       .then_inc(t_lo_done[u], 1)

            def project(r, u, w):
                dve.wait_ge(*proj_hi_done.at(u, r, HI[w]))
                hi, src, scale = place_of(u, w)
                lo = low_of(u, w)
                dve.scalar_tensor_tensor(lo, src, scale / WSCALE, hi, ALU.mult, ALU.subtract)\
                   .then_inc(proj_lo_done[u], 1)

            def scores(r, u, k):
                if k == 0:
                    dve.wait_ge(*masks_done.at(u, r, 1))
                    dve.wait_ge(*stored.before(u, r))
                dve.wait_ge(*scored.at(u, r, k))
                dve.tensor_tensor(score[u], blocks[u], (mask_bias if k < 2 else adj)[u][:, :].unsqueeze(1).unsqueeze(1)
                                  .broadcast_to([128, 2, DT, N]), ALU.add).then_inc(biased[u], 1)
                heads = slice(2 * (k % 2), 2 * (k % 2) + 2)
                dve.wait_ge(*biased.at(u, r, k))
                if k >= 2:
                    dve.tensor_reduce(low[u][:, heads, :], score[u], AX.X, ALU.min).then_inc(numbers[u], 1)
                    dve.wait_ge(*number(u, r, "minimum", k))
                dve.tensor_reduce(top[u][:, heads, :], score[u], AX.X, ALU.max, negate=True).then_inc(topped[u], 1)

            def turn_p(r, u, k):
                dve.wait_ge(*p_hi_done.at(u, r, k))
                dve.tensor_tensor(p_lo[u], blocks[u], p_hi[u], ALU.subtract).then_inc(p_lo_done[u], 1)

            def divide(r, u, k):
                o = b0[u][:, 0:2 * DT * HS].rearrange("p (g t c) -> p g t c", g=2, c=HS)
                heads = slice(2 * (k % 2), 2 * (k % 2) + 2)
                iv, fl = inv[u][:, heads, :], flag[u][:, heads, :]
                if k >= 2:
                    dve.wait_ge(*topped.at(u, r, k))
                    dve.tensor_scalar(fl, low[u][:, heads, :], 0.0, None, ALU.not_equal).then_inc(numbers[u], 1)
                    dve.wait_ge(*number(u, r, "low is not 0", k))
                    dve.scalar_tensor_tensor(fl, top[u][:, heads, :], 0.0, fl, ALU.not_equal, ALU.max)\
                       .then_inc(numbers[u], 1)
                dve.wait_ge(*attended.at(u, r, k))
                dve.reciprocal(iv, o[:, :, :, HD]).then_inc(numbers[u], 1)
                if k >= 2:
                    dve.wait_ge(*number(u, r, "inverse", k))
                    dve.tensor_tensor(iv, iv, fl, ALU.mult).then_inc(numbers[u], 1)
                dve.wait_ge(*number(u, r, "inverse" if k < 2 else "kept", k))
                dve.tensor_tensor(z[u][:, :].rearrange("p (t g c) -> p g t c", g=HG, c=HD)[:, heads, :, :],
                                  o[:, :, :, 0:HD], iv.unsqueeze(3).broadcast_to([128, 2, DT, HD]), ALU.mult)\
                   .then_inc(o_ready[u], 1)

            def u_gcn(r, u, layer):
                dve.wait_ge(*pair_done.at(u, r, 1))
                dve.wait_ge(*u_done.at(u, r, layer))
                dve.tensor_tensor(u_pair[u][:, :, :], b1[u][:, 0:2 * N].rearrange("p (a n) -> p a n", n=N),
                                  mask_pair[u][:, :, :], ALU.mult).then_inc(numbers[u], 1)
                dve.wait_ge(*number(u, r, "masked", layer))
                dve.tensor_tensor(e[u][:, :], u_pair[u][:, 0, :], u_pair[u][:, 1, :], ALU.add)\
                   .then_inc(u_ready[u], 1)

            def delta_gcn(r, u, layer):
                dve.wait_ge(*e_done.at(u, r, layer))
                dve.tensor_tensor(delta[u][:, :], e[u][:, :], adj_t[u][:, :], ALU.mult).then_inc(delta_done[u], 1)

            def u_di(r, u, layer):
                dve.wait_ge(*u_done.at(u, r, 2 + layer))
                dve.tensor_reduce(col(u, TOP), b1[u][:, 0:N], AX.X, ALU.max).then_inc(numbers[u], 1)
                dve.wait_ge(*number(u, r, "top of u", layer))
                dve.tensor_scalar(col(u, UBIAS), col(u, TOP), -1.0 / TEMPER, None, ALU.mult)\
                   .then_inc(u_bias_ready[u], 1)

            def delta_di(r, u, layer):
                dve.wait_ge(*e_done.at(u, r, 2 + layer))
                dve.tensor_tensor_reduce(out=delta[u][:, :], in0=e[u][:, :], in1=adj[u][:, :], scale=1.0,
                                         scalar=0.0, op0=ALU.mult, op1=ALU.add, accum_out=col(u, DSUM))\
                   .then_inc(delta_done[u], 1)

            def turn_delta(r, u, layer):
                dve.wait_ge(*turned.at(u, r, TURNED.index(("turn_delta", layer))))
                dve.tensor_tensor(delta3[u], b1[u][:, 0:N].unsqueeze(1).broadcast_to([128, 3, N]), tri[:, :, :],
                                  ALU.mult).then_inc(delta3_done[u], 1)

            def moments(r, u, step, src, between):
                n = 2 * MOMENTS.index(step)
                dve.bn_stats(st6[u][:, :], src).then_inc(moments_done[u], 1)
                dve.wait_ge(*moments_done.at(u, r, n))
                between()
                dve.bn_aggr(mv[u][:, :], st6[u][:, :]).then_inc(moments_done[u], 1)

            def inner(r, u, k):
                bank = (b1 if k < 2 else b0)[u]

                def between():
                    if k < 2:
                        dve.tensor_scalar(col(u, DENOM3), bank[:, D:D + 1], 1e-10, 1e-3, ALU.add, ALU.mult)\
                           .then_inc(numbers[u], 1)
                    else:
                        dve.tensor_copy(col(u, TICK), constant(HALF))

                dve.wait_ge(*mixed.at(u, r, k))
                moments(r, u, ("inner", k), bank[:, 0:D], between)
                dve.wait_ge(*moments_done.at(u, r, 2 * MOMENTS.index(("inner", k)) + 1))
                dve.scalar_tensor_tensor(zc[u], bank[:, 0:D], mv[u][:, 0:1], rows[:, 2 * k, :], ALU.subtract, ALU.mult)\
                   .then_inc(numbers[u], 1)

            def gain(r, u, k):
                dve.wait_ge(*root_done.at(u, r, ROOTS.index(("inner", k))))
                if k < 2:
                    dve.wait_ge(*number(u, r, "sum", k))
                    dve.scalar_tensor_tensor(col(u, BASE), col(u, ROOT), float(np.sqrt(D / (D - 1.0))), col(u, DENOM3),
                                             ALU.mult, ALU.add).then_inc(numbers[u], 1)
                    dve.wait_ge(*number(u, r, "gain base", k))
                    dve.reciprocal(col(u, GAIN), col(u, BASE)).then_inc(numbers[u], 1)
                    dve.wait_ge(*number(u, r, "gain", k))
                dve.wait_ge(*number(u, r, "centred", k))
                dve.scalar_tensor_tensor(z[u][:, :], zc[u], col(u, GAIN if k < 2 else ROOT), rows[:, 2 * k + 1, :],
                                         ALU.mult, ALU.add).then_inc(inner_done[u], 1)

            def residual(r, u, layer):
                if layer == 0:
                    dve.wait_ge(*x_biased.at(u, r, 0))
                    dve.wait_ge(*o_ready.at(u, r, 1))
                    dve.tensor_tensor(z[u][:, :], z[u][:, :], x[u][:, :], ALU.add).then_inc(residual_added[u], 1)
                elif layer < 3:
                    dve.wait_ge(*inner_done.at(u, r, 2 * layer - 1))
                    dve.scalar_tensor_tensor(z[u][:, :], z[u][:, :], 0.0, x[u][:, :], ALU.max, ALU.add)\
                       .then_inc(residual_added[u], 1)
                else:
                    dve.wait_ge(*x_biased.at(u, r, 1))
                    dve.wait_ge(*projected.at(u, r, ORDER[L3_O]))
                    dve.scalar_tensor_tensor(z[u][:, :], b1[u][:, 0:D], 1.0 / WSCALE, x[u][:, :], ALU.mult,
                                             ALU.add).then_inc(residual_added[u], 1)
                dve.wait_ge(*residual_added.at(u, r, layer))
                moments(r, u, ("residual", layer), z[u][:, :], lambda: dve.tensor_copy(col(u, TICK), constant(HALF)))

            def norm(r, u, layer):
                dve.wait_ge(*root_done.at(u, r, ROOTS.index(("residual", layer))))
                dve.tensor_scalar(out[u] if layer == 3 else x[u][:, :], z[u][:, :], mv[u][:, 0:1], col(u, ROOT), ALU.subtract, ALU.mult)\
                   .then_inc(normed[u], 1)

            dve.wait_ge(consts_made, 6)
            dve.wait_ge(small_loaded, 48)
            dve.wait_ge(dve_consts, DVE_CONSTS)

            def take(name, k, r, u):
                if name == "inner" and k == 0 and u == 0 and isinstance(r, int):
                    dve.wait_ge(rows_loaded, 16)
                {"weight": weight, "stages_free": stages_free, "masks": masks, "turn": turn, "project": project,
                 "scores": scores, "turn_p": turn_p, "divide": divide, "u_gcn": u_gcn, "delta_gcn": delta_gcn, "u_di": u_di, "delta_di": delta_di,
                 "turn_delta": turn_delta, "inner": inner, "gain": gain, "residual": residual,
                 "norm": norm}[name](r, u, k)

            rounds(dve, VECTOR, take)


def kernel(**inputs):
    import numpy as _np
    import concourse.bacc as _bacc
    from concourse.bass_utils import run_bass_kernel_spmd as _run

    a = {k: _np.asarray(v) for k, v in inputs.items()}
    ws = [a["L0_gnn_Wq"], a["L0_gnn_Wk"], a["L0_gnn_Wv"]]
    for layer in range(2):
        ws += [a[f"L1_gnn_{n}"][layer].T for n in ("W_left", "W_right", "W_lin")]
    for layer in range(2):
        ws += [a[f"L2_gnn_{n}"][layer].T for n in ("Wl", "Ws", "Wr")]
    ws += [a[f"L3_gnn_{n}"].T for n in ("Wq", "Wk", "Wv", "Wo")]
    biases = [a["L0_gnn_bq"], a["L0_gnn_bk"], a["L1_gnn_b_lin"][0], a["L1_gnn_b_lin"][1]]
    for layer in range(2):
        biases += [a[f"L2_gnn_{n}"][layer] for n in ("bl", "bs", "br")]
    biases += [a["L3_gnn_bv"]]
    rows = []
    for layer in range(2):
        rows += [a["L1_gnn_ln_a"][layer], a["L1_gnn_ln_b"][layer]]
    for layer in range(2):
        rows += [a["L2_gnn_ln_w"][layer], a["L2_gnn_ln_b"][layer]]
    rows += [a["L0_gnn_bv"], a["L3_gnn_bo"]]
    arrays = {
        "x_dram": _np.ascontiguousarray(a["x"]),
        "adj_dram": _np.ascontiguousarray(a["adj"]),
        "w_dram": _np.stack([_np.ascontiguousarray(w) for w in ws]),
        "bias_dram": _np.stack(biases),
        "rows_dram": _np.stack(rows),
        "beta_dram": a["L0_gnn_beta"].reshape(1),
    }
    nc = _bacc.Bacc("TRN2", target_bir_lowering=False, num_devices=1)
    args = [nc.dram_tensor(name, v.shape, F32, kind="ExternalInput").ap() for name, v in arrays.items()]
    out = nc.dram_tensor("out_dram", (B, N, D), F32, kind="ExternalOutput").ap()
    graph_layers(nc, *args, out)
    r = _run(nc, [arrays], core_ids=[0])
    return r.results[0]["out_dram"]
```
